# Optimizing a Trainium2 kernel written in Bass

```python
import numpy as np
import jax
import jax.numpy as jnp

def _softmax(x, axis=-1):
    return jax.nn.softmax(x, axis=axis)

def _gelu(x):
    return jax.nn.gelu(x, approximate=True)

def _silu(x):
    return jax.nn.silu(x)

def _sigmoid(x):
    return jax.nn.sigmoid(x)

def _layernorm(x, axis=-1, eps=1e-05):
    m = jnp.mean(x, axis=axis, keepdims=True)
    v = jnp.var(x, axis=axis, keepdims=True)
    return (x - m) / jnp.sqrt(v + eps)

def _scatter_add(tgt, idx, src, axis=0):
    return tgt.at[idx].add(src)

def _segment_sum(src, seg, n):
    return jax.ops.segment_sum(src, seg, n)
kernel_name = 'mk_gnn_ffn_d2_gnn_r8_6d7327'

def setup_inputs(seed: int=0):
    np.random.seed(seed)
    _w = jnp.asarray

    def _rec_inputs():
        import jax
        import jax.numpy as jnp
        _gk = jax.random.key(seed)
        x = -0.0006008 + 1.001 * jax.random.normal(jax.random.fold_in(_gk, 1), (6250, 256), jnp.float32)
        src = jax.random.randint(jax.random.fold_in(_gk, 2), (100000,), 0, 6250, jnp.int32)
        dst = jnp.minimum((6250 * jax.random.uniform(jax.random.fold_in(_gk, 3), (100000,)) ** 2.0).astype(jnp.int32), 49999)
        _o = jnp.argsort(dst, stable=True)
        src = src[_o]
        dst = dst[_o]
        edge_type_16 = jax.random.randint(jax.random.fold_in(_gk, 12), (100000,), 0, 16, jnp.int32)
        return (x, src, dst, edge_type_16)
    x, src, dst, edge_type_16 = _rec_inputs()

    def _L0_gnn_setup():
        import jax, jax.numpy as jnp
        import numpy as np
        N_NODES = 1250
        N_EDGES = 40000
        IN_DIM = 256
        OUT_DIM = 256
        N_REL = 16
        key = jax.random.key(seed)
        k_x, k_src, k_dst, k_et, k_wr, k_w0 = jax.random.split(key, 6)
        x = jax.random.normal(k_x, (N_NODES, IN_DIM), dtype=jnp.float32)
        src = jax.random.randint(k_src, (N_EDGES,), 0, N_NODES)
        dst = jax.random.randint(k_dst, (N_EDGES,), 0, N_NODES)
        edge_index = jnp.stack([src, dst], axis=0)
        edge_type = jax.random.randint(k_et, (N_EDGES,), 0, N_REL)
        lim_r = float(np.sqrt(6.0 / (IN_DIM + OUT_DIM)))
        W_r = jax.random.uniform(k_wr, (N_REL, IN_DIM, OUT_DIM), minval=-lim_r, maxval=lim_r, dtype=jnp.float32)
        W0_w = jax.random.uniform(k_w0, (OUT_DIM, IN_DIM), minval=-lim_r, maxval=lim_r, dtype=jnp.float32)
        W0_b = jnp.zeros((OUT_DIM,), dtype=jnp.float32)
        return {'x': x, 'W_r': W_r, 'W0_w': W0_w, 'W0_b': W0_b, 'edge_index': edge_index, 'edge_type': edge_type, 'num_nodes_local': N_NODES}
    _L0_gnn_all = _L0_gnn_setup()
    _L0_gnn_in = {k: v for k, v in _L0_gnn_all.items() if k in ('W_r', 'W0_w', 'W0_b')}
    del _L0_gnn_all

    def _L0_ffn_setup():
        import math
        import jax, jax.numpy as jnp
        import numpy as np
        CAPACITY_FACTOR = 1.25
        key = jax.random.key(seed)
        ks = jax.random.split(key, 5)
        B, L, D, F, E = (8, 1024, 256, 1024, 8)
        h = jax.random.normal(ks[0], (B, L, D), dtype=jnp.float32)
        gate_w = jax.random.normal(ks[1], (D, E), dtype=jnp.float32) * 0.02
        gate_b = jnp.zeros((E,), dtype=jnp.float32)
        w1 = jax.random.normal(ks[2], (E, D, F), dtype=jnp.float32) * (1.0 / math.sqrt(D))
        b1 = jnp.zeros((E, F), dtype=jnp.float32)
        w2 = jax.random.normal(ks[3], (E, F, D), dtype=jnp.float32) * (1.0 / math.sqrt(F))
        b2 = jnp.zeros((E, D), dtype=jnp.float32)
        return {'h': h, 'gate_w': gate_w, 'gate_b': gate_b, 'w1': w1, 'b1': b1, 'w2': w2, 'b2': b2}
    _L0_ffn_all = _L0_ffn_setup()
    _L0_ffn_in = {k: v for k, v in _L0_ffn_all.items() if k in ('gate_w', 'gate_b', 'w1', 'b1', 'w2', 'b2')}
    del _L0_ffn_all

    def _L1_gnn_setup():
        import jax, jax.numpy as jnp
        import numpy as np
        N_NODES = 12500
        N_EDGES = 400000
        D_IN = 256
        D_OUT = 256
        key = jax.random.key(seed)
        k1, k2, k3, k4 = jax.random.split(key, 4)
        x = jax.random.normal(k1, (N_NODES, D_IN), dtype=jnp.float32)
        edge_index = jax.random.randint(k2, (2, N_EDGES), 0, N_NODES, dtype=jnp.int64)
        limit = np.sqrt(6.0 / (D_IN + D_OUT)).astype(np.float32)
        W = jax.random.uniform(k3, (D_IN, D_OUT), dtype=jnp.float32, minval=-limit, maxval=limit)
        b = jnp.zeros((D_OUT,), dtype=jnp.float32)
        return {'x': x, 'edge_index': edge_index, 'W': W, 'b': b}
    _L1_gnn_all = _L1_gnn_setup()
    _L1_gnn_in = {k: v for k, v in _L1_gnn_all.items() if k in ('W', 'b')}
    del _L1_gnn_all

    def _L1_ffn_setup():
        import jax, jax.numpy as jnp
        import numpy as np
        B, T, D, H, L = (16, 512, 256, 256, 2)

        def _lstm(x, W_ih, W_hh, b_ih, b_hh):
            x_proj = jnp.einsum('btd,gd->btg', x, W_ih) + b_ih + b_hh
            h0 = jnp.zeros((x.shape[0], W_hh.shape[1]), x.dtype)
            c0 = jnp.zeros_like(h0)

            def step(carry, xp):
                h, c = carry
                gates = xp + h @ W_hh.T
                i, f, g, o = jnp.split(gates, 4, axis=-1)
                c = jax.nn.sigmoid(f) * c + jax.nn.sigmoid(i) * jnp.tanh(g)
                h = jax.nn.sigmoid(o) * jnp.tanh(c)
                return ((h, c), h)
            _, hs = jax.lax.scan(step, (h0, c0), jnp.swapaxes(x_proj, 0, 1))
            return jnp.swapaxes(hs, 0, 1)
        key = jax.random.key(seed)
        ks = jax.random.split(key, 9)
        s = 1.0 / np.sqrt(H)
        u = lambda k, shape: jax.random.uniform(k, shape, jnp.float32, -s, s)
        return {'x': jax.random.normal(ks[0], (B, T, D), jnp.float32), 'W_ih': u(ks[1], (4 * H, D)), 'W_hh': u(ks[2], (4 * H, H)), 'b_ih': u(ks[3], (4 * H,)), 'b_hh': u(ks[4], (4 * H,)), 'W_lin': u(ks[5], (L, H)), 'b_lin': u(ks[6], (L,)), 'fw_att': jnp.full((1, H), 0.001, jnp.float32), 'bw_att': jnp.full((1, H), 0.001, jnp.float32)}
    _L1_ffn_all = _L1_ffn_setup()
    _L1_ffn_in = {k: v for k, v in _L1_ffn_all.items() if k in ('W_ih', 'W_hh', 'b_ih', 'b_hh', 'W_lin', 'b_lin', 'fw_att', 'bw_att')}
    del _L1_ffn_all
    return {'x': x, 'src': src, 'dst': dst, 'edge_type_16': edge_type_16, 'L0_gnn_W_r': _L0_gnn_in['W_r'], 'L0_gnn_W0_w': _L0_gnn_in['W0_w'], 'L0_gnn_W0_b': _L0_gnn_in['W0_b'], 'L0_ffn_gate_w': _L0_ffn_in['gate_w'], 'L0_ffn_gate_b': _L0_ffn_in['gate_b'], 'L0_ffn_w1': _L0_ffn_in['w1'], 'L0_ffn_b1': _L0_ffn_in['b1'], 'L0_ffn_w2': _L0_ffn_in['w2'], 'L0_ffn_b2': _L0_ffn_in['b2'], 'L1_gnn_W': _L1_gnn_in['W'], 'L1_gnn_b': _L1_gnn_in['b'], 'L1_ffn_W_ih': _L1_ffn_in['W_ih'], 'L1_ffn_W_hh': _L1_ffn_in['W_hh'], 'L1_ffn_b_ih': _L1_ffn_in['b_ih'], 'L1_ffn_b_hh': _L1_ffn_in['b_hh'], 'L1_ffn_W_lin': _L1_ffn_in['W_lin'], 'L1_ffn_b_lin': _L1_ffn_in['b_lin'], 'L1_ffn_fw_att': _L1_ffn_in['fw_att'], 'L1_ffn_bw_att': _L1_ffn_in['bw_att']}

def reference(x, src, dst, edge_type_16, L0_gnn_W_r, L0_gnn_W0_w, L0_gnn_W0_b, L0_ffn_gate_w, L0_ffn_gate_b, L0_ffn_w1, L0_ffn_b1, L0_ffn_w2, L0_ffn_b2, L1_gnn_W, L1_gnn_b, L1_ffn_W_ih, L1_ffn_W_hh, L1_ffn_b_ih, L1_ffn_b_hh, L1_ffn_W_lin, L1_ffn_b_lin, L1_ffn_fw_att, L1_ffn_bw_att):
    import jax
    import jax.numpy as jnp

    def _L0_gnn_ref(x, W_r, W0_w, W0_b, edge_index, edge_type, num_nodes_local):
        import jax, jax.numpy as jnp
        import numpy as np
        N_NODES = 1250
        N_EDGES = 40000
        IN_DIM = 256
        OUT_DIM = 256
        N_REL = 16
        N = num_nodes_local
        R = W_r.shape[0]
        src = edge_index[0]
        dst = edge_index[1]
        deg = jnp.zeros((R, N), dtype=x.dtype).at[edge_type, dst].add(1.0)
        deg = jnp.maximum(deg, 1.0)
        h_all = jnp.einsum('nd,rdo->rno', x, W_r)
        msg = h_all[edge_type, src] / deg[edge_type, dst][:, None]
        agg = jax.ops.segment_sum(msg, dst, num_segments=N)
        return agg + x @ W0_w.T + W0_b

    def _L0_ffn_ref(h, gate_w, gate_b, w1, b1, w2, b2):
        import math
        import jax, jax.numpy as jnp
        import numpy as np
        CAPACITY_FACTOR = 1.25
        B, L, D = h.shape
        E = gate_w.shape[1]
        T = B * L
        C = max(1, math.ceil(CAPACITY_FACTOR * T / E))
        x = h.reshape(T, D)
        logits = x @ gate_w + gate_b
        probs = jax.nn.softmax(logits, axis=-1)
        idx = jnp.argmax(probs, axis=-1)
        prb = jnp.take_along_axis(probs, idx[:, None], axis=1)[:, 0]
        one_hot = jax.nn.one_hot(idx, E, dtype=jnp.float32)
        pos = (jnp.cumsum(one_hot, axis=0) * one_hot).sum(-1).astype(jnp.int32) - 1
        kept = pos < C
        pos_safe = jnp.where(kept, pos, C)
        buf = jnp.zeros((E, C, D), dtype=h.dtype).at[idx, pos_safe].set(x, mode='drop')
        hmid = jax.nn.relu(jnp.einsum('ecd,edf->ecf', buf, w1) + b1[:, None, :])
        ybuf = jnp.einsum('ecf,efd->ecd', hmid, w2) + b2[:, None, :]
        pos_g = jnp.minimum(pos, C - 1)
        y_tok = ybuf[idx, pos_g] * (prb * kept)[:, None]
        y = y_tok.reshape(B, L, D)
        y = jnp.nan_to_num(y, nan=0.0, posinf=10000.0, neginf=-10000.0)
        return y

    def _L1_gnn_ref(x, edge_index, W, b):
        import jax, jax.numpy as jnp
        import numpy as np
        N_NODES = 12500
        N_EDGES = 400000
        D_IN = 256
        D_OUT = 256
        N = x.shape[0]
        h = x @ W
        loop = jnp.arange(N, dtype=edge_index.dtype)
        src = jnp.concatenate([edge_index[0], loop])
        dst = jnp.concatenate([edge_index[1], loop])
        deg = jax.ops.segment_sum(jnp.ones(dst.shape, dtype=h.dtype), dst, num_segments=N)
        dinv = jnp.where(deg > 0, jax.lax.rsqrt(deg), 0.0)
        norm = dinv[src] * dinv[dst]
        out = jax.ops.segment_sum(norm[:, None] * h[src], dst, num_segments=N) + b
        return jax.nn.leaky_relu(out, negative_slope=0.2)

    def _L1_ffn_ref(x, W_ih, W_hh, b_ih, b_hh, W_lin, b_lin, fw_att, bw_att):
        import jax, jax.numpy as jnp
        import numpy as np
        B, T, D, H, L = (16, 512, 256, 256, 2)

        def _lstm(x, W_ih, W_hh, b_ih, b_hh):
            x_proj = jnp.einsum('btd,gd->btg', x, W_ih) + b_ih + b_hh
            h0 = jnp.zeros((x.shape[0], W_hh.shape[1]), x.dtype)
            c0 = jnp.zeros_like(h0)

            def step(carry, xp):
                h, c = carry
                gates = xp + h @ W_hh.T
                i, f, g, o = jnp.split(gates, 4, axis=-1)
                c = jax.nn.sigmoid(f) * c + jax.nn.sigmoid(i) * jnp.tanh(g)
                h = jax.nn.sigmoid(o) * jnp.tanh(c)
                return ((h, c), h)
            _, hs = jax.lax.scan(step, (h0, c0), jnp.swapaxes(x_proj, 0, 1))
            return jnp.swapaxes(hs, 0, 1)
        lstm_out = _lstm(x, W_ih, W_hh, b_ih, b_hh)
        logits = jnp.einsum('bth,lh->btl', lstm_out, W_lin) + b_lin
        g = jax.lax.stop_gradient(jnp.argmax(logits, axis=-1).astype(lstm_out.dtype))[..., None]
        w = g * lstm_out
        inc = jnp.cumsum(w, axis=1)
        prefix = inc - w
        suffix = inc[:, -1:, :] - inc
        return 2.0 * lstm_out + prefix * fw_att + suffix * bw_att
    edge_index = jnp.stack([src, dst])
    x = x + _L0_gnn_ref(_layernorm(x, axis=-1), L0_gnn_W_r, L0_gnn_W0_w, L0_gnn_W0_b, edge_index, edge_type_16, 6250)
    x = x + _L0_ffn_ref(_layernorm(x, axis=-1)[None], L0_ffn_gate_w, L0_ffn_gate_b, L0_ffn_w1, L0_ffn_b1, L0_ffn_w2, L0_ffn_b2)[0]
    x = x + _L1_gnn_ref(_layernorm(x, axis=-1), edge_index, L1_gnn_W, L1_gnn_b)
    x = x + _L1_ffn_ref(_layernorm(x, axis=-1)[None], L1_ffn_W_ih, L1_ffn_W_hh, L1_ffn_b_ih, L1_ffn_b_hh, L1_ffn_W_lin, L1_ffn_b_lin, L1_ffn_fw_att, L1_ffn_bw_att)[0]
    return x

_drawn_inputs = setup_inputs


def setup_inputs(seed=0):
    import zlib

    import numpy as np

    out = dict(_drawn_inputs(seed))
    spreads = {'L0_gnn_W0_b': (0.0, 0.1),
     'L0_ffn_gate_b': (0.0, 0.1),
     'L0_ffn_b1': (0.0, 0.8),
     'L0_ffn_b2': (0.0, 0.8),
     'L1_gnn_b': (0.0, 0.315),
     'L1_ffn_fw_att': (0.0010000000474974513, 0.6),
     'L1_ffn_bw_att': (0.0010000000474974513, 0.6)}
    factors = {'L1_ffn_W_hh': 3.288,
     'L1_ffn_b_ih': 4.069,
     'L1_ffn_b_hh': 3.713,
     'L1_ffn_W_lin': 7.609,
     'L1_ffn_b_lin': 3.388}
    for name, (base, spread) in spreads.items():
        noise = np.random.default_rng([zlib.crc32(name.encode()), seed]).standard_normal(out[name].shape)
        drawn = base * np.exp(spread * noise) if base else spread * noise
        out[name] = jnp.asarray(drawn.astype(out[name].dtype))
    for name, factor in factors.items():
        out[name] = (out[name] * factor).astype(out[name].dtype)
    return out
```

```python
from contextlib import ExitStack

import concourse.bass as bass
from concourse import mybir

P = 128
F32 = mybir.dt.float32
BF16 = mybir.dt.bfloat16
I32 = mybir.dt.int32
U32 = mybir.dt.uint32
U8 = mybir.dt.uint8
ALU = mybir.AluOpType
ACT = mybir.ActivationFunctionType
AX = mybir.AxisListType.X

EPS = 1e-5
WIN = 128
PER = 4
EG = PER * P
FAST_PASSES = 3
TOL = 2.0 ** -20


class K:

    def sem(self, name):
        sem = self.nc.alloc_semaphore(name=name)
        self.stage_sems.append(sem)
        return sem

    def pool_dma_sem(self, name):
        if self.pool_dma_used == len(self.pool_dma_sems):
            self.pool_dma_sems.append(self.nc.alloc_semaphore(name=f"pool_dma{self.pool_dma_used}"))
        self.pool_dma_used += 1
        return self.pool_dma_sems[self.pool_dma_used - 1]

    def end_stage(self):
        clear(self, self.stage_sems + self.pool_dma_sems)
        for sem in self.stage_sems:
            self.nc.release_semaphore(sem)
        self.stage_sems = []
        self.pool_dma_used = 0


def rest(k, eng, sem, value):
    eng.wait_ge(sem, value)


def hold(k, eng, sem, value):
    eng.wait_ge(sem, value)
    eng.sem_inc(k.s_seen, 1)


def prime(k, eng, sems):
    for sem in sems:
        eng.dma_start(k.primed[k.n_primed:k.n_primed + 1], k.zero[0:1, 0:16]).then_inc(sem, 16)
        k.n_primed += 1


class Chain:

    def __init__(self, eng, sem, k=None, first=0, wait=rest):
        self.eng, self.sem, self.k, self.n, self.first, self.wait = eng, sem, k, 0, first, wait

    def __call__(self, ins):
        self.n += 1
        ins.then_inc(self.sem, 1)
        self.wait(self.k, self.eng, self.sem, self.first + self.n)


class LayerNorm:

    def __init__(self, k, sb):
        self.k = k
        self.s_step, self.s_var, self.s_std = (k.sem(n) for n in ("ln_step", "ln_var", "ln_std"))
        self.stats, self.mv, self.rstd = sb("ln_stats", [P, 6], F32), sb("ln_mv", [P, 2], F32), sb("ln_rstd", [P, 2], F32)

    def rows(self, v, t, x, out):
        k, rstd = self.k, self.rstd
        link = Chain(v, self.s_step, k, 3 * t, hold)
        link(v.bn_stats(self.stats[:], x))
        v.bn_aggr(self.mv[:], self.stats[:]).then_inc(self.s_var, 1)
        rest(k, v, self.s_std, t + 1)
        link(v.reciprocal(rstd[:, 1:2], rstd[:, 0:1]))
        link(v.tensor_scalar(out, x, self.mv[:, 0:1], rstd[:, 1:2], ALU.subtract, ALU.mult))

    def root(self, act, t):
        rest(self.k, act, self.s_var, t + 1)
        act.activation(self.rstd[:, 0:1], self.mv[:, 1:2], ACT.Sqrt, bias=self.k.eps[:, 0:1]).then_inc(self.s_std, 1)


def stage_constants(k):
    nc = k.nc
    with nc.Block() as block:
        @block.gpsimd
        def _(pool):
            link = Chain(pool, k.sem("c_pool"))
            link(pool.iota(k.iota_i[:], pattern=[[1, P]], base=0, channel_multiplier=0))
            link(pool.iota(k.part_i[:], pattern=[[1, 1]], base=0, channel_multiplier=1))
            link(pool.tensor_copy(k.iota[:], k.iota_i[:]))
            link(pool.tensor_copy(k.part[:], k.part_i[:]))
            link(pool.memset(k.ones[:], 1.0))
            link(pool.memset(k.zero[:], 0.0))
            link(pool.memset(k.eps[:], EPS))
            link(pool.affine_select(out=k.ident[:], in_=k.ones[:], compare_op=ALU.is_equal, fill=0.0,
                                    base=0, pattern=[[1, P]], channel_multiplier=-1))
            link(pool.affine_select(out=k.upper[:], in_=k.ones[:], compare_op=ALU.is_ge, fill=0.0,
                                    base=0, pattern=[[1, P]], channel_multiplier=-1))
            link(pool.affine_select(out=k.strict[:], in_=k.ones[:], compare_op=ALU.is_gt, fill=0.0,
                                    base=0, pattern=[[1, P]], channel_multiplier=-1))


def stage_edges(k, x, src, dst, etype):
    nc, NG = k.nc, k.NG
    H = NG // 2
    full = k.E // EG
    tail = k.E - full * EG
    s_fill, s_ld, s_cv, s_tp, s_ev, s_dv, s_pe, s_pad = (
        k.sem(n) for n in ("e_fill", "e_ld", "e_cv", "e_tp", "e_ev", "e_dv", "e_pe", "e_pad"))
    with ExitStack() as st:
        sb = lambda n, s, d: st.enter_context(nc.sbuf_tensor(n, s, d))
        raw = sb("e_raw", [H, 3, 2, EG], I32)
        rawf = sb("e_rawf", [H, 3, 2, EG], F32)
        base_i = sb("e_base_i", [1, NG], I32)
        base_f = sb("e_base_f", [1, NG], F32)
        base_b = sb("e_base_b", [P, NG], F32)
        srcf = sb("e_srcf", [P, NG, PER], F32)
        t1 = sb("e_t1", [P, NG * PER], F32)
        t2 = sb("e_t2", [P, NG * PER], F32)
        bad = sb("e_bad", [P, 2], F32)
        zpad = sb("e_zpad", [P, 3072], F32)
        ps = st.enter_context(nc.psum_tensor("e_ps", [P, 2, 512], F32))
        with nc.Block() as block:
            @block.gpsimd
            def _(pool):
                pool.memset(raw[:, 0], -1).then_inc(s_fill, 1)
                pool.memset(raw[:, 1:3], 0).then_inc(s_fill, 1)
                pool.memset(zpad[:], 0.0).then_inc(s_fill, 1)

            @block.sync
            def _(sp):
                sp.wait_ge(s_fill, 3)
                n = 0
                for a, v in enumerate((dst, src, etype)):
                    rows = v[0:full * EG].rearrange("(g e) -> g e", e=EG)
                    sp.dma_start(raw[:, a, 0], rows[0:H]).then_inc(s_ld, 16)
                    sp.dma_start(raw[0:full - H, a, 1], rows[H:full]).then_inc(s_ld, 16)
                    sp.dma_start(raw[full - H:full - H + 1, a, 1, 0:tail],
                                 v[full * EG:k.E].rearrange("(o e) -> o e", o=1)).then_inc(s_ld, 16)
                firsts = bass.AP(tensor=dst.tensor, offset=0, ap=[[0, 1], [EG, NG]])
                with nc.allow_non_contiguous_dma("one edge of each group"):
                    sp.dma_start(base_i[:], firsts).then_inc(s_ld, 16)
                sp.dma_start(k.xpad[0:k.N], x).then_inc(s_pad, 16)
                half = (k.NP - k.N) // 2
                sp.dma_start(k.xpad[k.N:k.NP].rearrange("(p a) d -> p (a d)", a=2),
                             zpad[0:half, 0:2 * k.D]).then_inc(s_pad, 16)
                sp.dma_start(k.typ[0:k.E].rearrange("(a b) -> a b", a=16),
                             etype.rearrange("(a b) -> a b", a=16)).then_inc(s_pad, 16)
                npad = NG * EG - k.E
                sp.dma_start(k.typ[k.E:].rearrange("(a b) -> a b", a=32),
                             zpad[0:32, 0:npad // 32].bitcast(I32)).then_inc(s_pad, 16)
                per = k.EX * k.CS * k.D // P // 8
                rows = k.buf[0:k.EX * k.CS].rearrange("(b p a) d -> b p (a d)", p=P, b=8)
                for b in range(8):
                    sp.dma_start(rows[b], zpad[:, 0:per]).then_inc(s_pad, 16)
                sp.wait_ge(s_pad, 12 * 16)

            @block.tensor
            def _(pe):
                for a in range(3):
                    pe.wait_ge(s_cv, a + 1)
                    for j in range(PER):
                        n = a * PER + j
                        if n >= 2:
                            pe.wait_ge(s_ev, n - 1)
                        for h in range(2):
                            mm = pe.transpose(ps[:, n % 2, h * H:(h + 1) * H],
                                              rawf[:, a, h, j * P:(j + 1) * P], k.ident[0:H, 0:H])
                        mm.then_inc(s_tp, 1)
                pe.wait_ge(s_ev, 3 * PER)
                pe.wait_ge(s_dv, 2)
                pe.matmul(ps[:, 0, 0:NG], k.ones[0:1, :], base_f[:], start=True, stop=True).then_inc(s_pe, 1)
                pe.wait_ge(s_dv, 9)
                pe.matmul(ps[:, 1, 0:2], k.ones[:, :], bad[:], start=True, stop=True).then_inc(s_pe, 1)

            @block.vector
            def _(v):
                v.wait_ge(s_ld, 16 * 10)
                for a in range(3):
                    v.tensor_copy(rawf[:, a], raw[:, a]).then_inc(s_cv, 1)
                for a, to in enumerate((k.dstf, srcf, k.typf)):
                    for j in range(PER):
                        n = a * PER + j
                        v.wait_ge(s_tp, n + 1)
                        v.tensor_copy(to[:, :, j], ps[:, n % 2, 0:NG]).then_inc(s_ev, 1)
                v.wait_ge(s_ev, 3 * PER)
                link = Chain(v, s_dv)
                link(v.tensor_copy(base_f[:], base_i[:]))
                link(v.tensor_scalar(base_f[:], base_f[:], float(k.NP - WIN), None, ALU.min))
                v.wait_ge(s_pe, 1)
                link(v.tensor_copy(base_b[:], ps[:, 0, 0:NG]))
                link(v.tensor_copy(k.base[:], base_f[:]))
                link(v.tensor_tensor(k.rel[:], k.dstf[:],
                                     base_b[:].rearrange("p (g o) -> p g o", o=1).broadcast_to([P, NG, PER]),
                                     ALU.subtract))
                rel = k.rel[:].rearrange("p g j -> p (g j)")
                dstv = k.dstf[:].rearrange("p g j -> p (g j)")
                link(v.tensor_scalar(t1[:], rel, 0.0, None, ALU.is_lt))
                link(v.scalar_tensor_tensor(out=t2[:], in0=dstv, scalar=0.0, in1=t1[:],
                                            op0=ALU.is_ge, op1=ALU.mult))
                link(v.tensor_reduce(bad[:, 0:1], t2[:], AX, ALU.add))
                v.tensor_scalar(t1[:], rel, float(WIN - 1), None, ALU.is_gt).then_inc(s_cv, 1)
                v.wait_ge(s_cv, 4)
                link(v.tensor_reduce(bad[:, 1:2], t1[:], AX, ALU.add))
                v.wait_ge(s_pe, 2)
                link(v.tensor_tensor(bad[0:1, 0:1], ps[0:1, 1, 0:1], k.zero[0:1, 0:1], ALU.add))
                link(v.tensor_tensor(bad[0:1, 0:1], ps[0:1, 1, 1:2], bad[0:1, 0:1], ALU.add))
                link(v.tensor_scalar(bad[0:1, 0:1], bad[0:1, 0:1], 0.0, None, ALU.is_gt))
                link(v.tensor_copy(k.scattered[:], bad[0:1, 0:1]))
                link(v.tensor_copy(k.src_row[:], srcf[:]))
                link(v.scalar_tensor_tensor(out=t1[:], in0=srcf[:].rearrange("p g j -> p (g j)"),
                                            scalar=float(k.R), in1=k.typf[:].rearrange("p g j -> p (g j)"),
                                            op0=ALU.mult, op1=ALU.add))
                link(v.tensor_copy(k.rel_row[:].rearrange("p g j -> p (g j)"), t1[:]))


def for_windows(k, name, run):
    nc = k.nc
    with nc.If(nc.values_load(k.scattered[0:1, 0:1], min_val=0, max_val=1) > 0):
        with nc.Fori(0, k.NP // WIN) as w:
            with nc.Block() as block:
                @block.gpsimd
                def _(pool):
                    pool.iota(k.win_i[:], pattern=[[1, 1]], base=0, channel_multiplier=0).then_inc(k.s_win, 1)
                    pool.wait_ge(k.s_win, 1)

                @block.vector
                def _(v):
                    v.wait_ge(k.s_win, 1)
                    v.tensor_scalar(k.rel[:], k.dstf[:], k.win_f[:, 0:1], None, ALU.subtract).then_inc(k.s_win, 1)
                    v.wait_ge(k.s_win, 2)
                    v.tensor_scalar(k.win_f[:], k.win_f[:], float(WIN), None, ALU.add).then_inc(k.s_win, 1)
                    v.wait_ge(k.s_win, 3)
            run(w * WIN)
            nc.gpsimd.sem_clear(k.s_win)
            nc.all_engine_barrier()
    with nc.Else():
        run(None)
    nc.all_engine_barrier()


def clear(k, sems):
    k.nc.gpsimd.dma_reset()
    for s in sems:
        k.nc.gpsimd.sem_clear(s)
    k.nc.all_engine_barrier()


def stage_degrees(k):
    nc, NG = k.nc, k.NG
    s_p, s_mm, s_add = (k.sem(n) for n in ("d_p", "d_mm", "d_add"))
    sems = (s_p, s_mm, s_add)
    with ExitStack() as st:
        sb = lambda n, s, d: st.enter_context(nc.sbuf_tensor(n, s, d))
        hit = sb("d_hit", [P, 2, PER, WIN], BF16)
        hot = sb("d_hot", [P, 2, PER, k.R], BF16)
        ps = st.enter_context(nc.psum_tensor("d_ps", [k.R, 2, 512], F32))

        def run(fixed):
            with nc.Block() as block:
                @block.vector
                def _(v):
                    def build(g, u):
                        v.tensor_tensor(hit[:, u],
                                        k.iota[:].rearrange("p (o w) -> p o w", o=1).broadcast_to([P, PER, WIN]),
                                        k.rel[:, bass.ds(g, 1), :].rearrange("p o (j q) -> p (o j) q", q=1)
                                        .broadcast_to([P, PER, WIN]), ALU.is_equal).then_inc(s_p, 1)
                        v.tensor_tensor(hot[:, u],
                                        k.iota[:, 0:k.R].rearrange("p (o w) -> p o w", o=1)
                                        .broadcast_to([P, PER, k.R]),
                                        k.typf[:, bass.ds(g, 1), :].rearrange("p o (j q) -> p (o j) q", q=1)
                                        .broadcast_to([P, PER, k.R]), ALU.is_equal).then_inc(s_p, 1)

                    def add(g, u):
                        at = (v.value_load(k.base[0:1, bass.ds(g, 1)], min_val=0, max_val=k.NP - WIN)
                              if fixed is None else fixed)
                        v.wait_ge(s_mm, g + 1)
                        v.wait_ge(s_add, g + 2)
                        v.tensor_tensor(k.degT[:, bass.ds(at, WIN)], k.degT[:, bass.ds(at, WIN)],
                                        ps[:, u, 0:WIN], ALU.add).then_inc(s_add, 1)

                    v.sem_inc(s_add, 2)
                    build(0, 0)
                    with v.Fori(0, NG // 2 - 1) as i:
                        for u in range(2):
                            build(2 * i + u + 1, 1 - u)
                            add(2 * i + u, u)
                    build(NG - 1, 1)
                    add(NG - 2, 0)
                    add(NG - 1, 1)
                    v.wait_ge(s_add, NG + 2)

                @block.tensor
                def _(pe):
                    pe.wait_ge(s_add, 1)
                    with pe.Fori(0, NG // 2) as i:
                        for u in range(2):
                            g = 2 * i + u
                            pe.wait_ge(s_p, 2 * g + 2)
                            pe.wait_ge(s_add, g + 1)
                            for j in range(PER):
                                mm = pe.matmul(ps[:, u, 0:WIN], hot[:, u, j], hit[:, u, j],
                                               start=(j == 0), stop=(j == PER - 1))
                            mm.then_inc(s_mm, 1)
            clear(k, sems)

        with nc.Block() as block:
            @block.vector
            def _(v):
                link = Chain(v, k.sem("d_z"))
                link(v.memset(k.degT[:], 0.0))
                link(v.memset(k.win_f[:], 0.0))
        for_windows(k, "deg", run)

        s_row, s_c, s_rt = k.sem("d_row"), k.sem("d_c"), k.sem("d_rt")
        psr = st.enter_context(nc.psum_tensor("d_psr", [P, 512], F32))
        with nc.Block() as block:
            @block.tensor
            def _(pe):
                for t in range(k.NT):
                    mm = pe.matmul(psr[:, t:t + 1], k.degT[:, t * P:(t + 1) * P], k.ones[0:k.R, 0:1],
                                   start=True, stop=True)
                mm.then_inc(s_row, 1)

            @block.scalar
            def _(act):
                act.wait_ge(s_c, 1)
                act.activation(k.dinv[:], k.dinv[:], ACT.Sqrt).then_inc(s_rt, 1)

            @block.vector
            def _(v):
                link = Chain(v, s_c)
                v.wait_ge(s_row, 1)
                link(v.tensor_scalar(k.dinv[:], psr[:, 0:k.NT], 1.0, None, ALU.add))
                v.wait_ge(s_rt, 1)
                link(v.reciprocal(k.dinv[:], k.dinv[:]))
                link(v.tensor_scalar(k.degT[:], k.degT[:], 1.0, None, ALU.max))
                link(v.reciprocal(k.degT[:], k.degT[:]))


def stage_relations(k, W_r, W0_w, W0_b):
    nc, D, R = k.nc, k.D, k.R
    NC = R * D // 512
    nm = ("r_w", "r_w0", "r_w0t", "r_w0c", "r_x0", "r_x1", "r_ln", "r_xn", "r_tp", "r_xt", "r_mm",
          "r_ea", "r_ed", "r_b", "r_b1", "r_h0", "r_h1", "r_o0", "r_o1")
    (s_w, s_w0, s_w0t, s_w0c, s_x0, s_x1, s_ln, s_xn, s_tp, s_xt, s_mm, s_ea, s_ed, s_b, s_b1,
     s_h0, s_h1, s_o0, s_o1) = (k.pool_dma_sem(n) if n in nm[-4:] else k.sem(n) for n in nm)
    s_x, s_h, s_o = (s_x0, s_x1), (s_h0, s_h1), (s_o0, s_o1)
    with ExitStack() as st:
        sb = lambda n, s, d: st.enter_context(nc.sbuf_tensor(n, s, d))
        ps_ = lambda n, s: st.enter_context(nc.psum_tensor(n, s, F32))
        w = sb("r_W", [P, 2, R * D], F32)
        w0raw = sb("r_W0raw", [P, 2, D], F32)
        w0 = sb("r_W0", [P, 2, D], F32)
        bias = sb("r_bias", [P, D], F32)
        xt = sb("r_xt_", [P, 2, D], F32)
        ln = LayerNorm(k, sb)
        xn = sb("r_xn_", [P, 2, D], F32)
        xnT = sb("r_xnT", [P, 2, 2, P], F32)
        hst = sb("r_hst", [P, 2, R * D], F32)
        bst = sb("r_bst", [P, 2, D], F32)
        pst = ps_("r_pst", [P, 2, 2, P])
        psm = ps_("r_psm", [P, 4, 512])
        psb = ps_("r_psb", [P, 2, 512])
        rows_x = k.xpad
        with nc.Block() as block:
            @block.sync
            def _(sp):
                for r in range(R):
                    sp.dma_start(w[:, :, r * D:(r + 1) * D], W_r[r].rearrange("(k p) o -> p k o", p=P)).then_inc(s_w, 16)
                sp.dma_start(w0raw[:], W0_w.rearrange("(a p) i -> p a i", p=P)).then_inc(s_w0, 16)
                sp.dma_start(bias[:], W0_b.partition_broadcast(P)).then_inc(s_w0, 16)
                with sp.Fori(0, k.NT // 2) as i:
                    for u in range(2):
                        rest(k, sp, s_b, 2 * i + u + 1)
                        sp.dma_start(xt[:, u], rows_x[bass.ds((2 * i + u) * P, P)]).then_inc(s_x[u], 16)

            @block.vector
            def _(v):
                v.sem_inc(s_b, 2)
                v.sem_inc(s_ed, 2)
                for kk in range(2):
                    v.wait_ge(s_w0t, kk + 1)
                    v.tensor_copy(w0[:, kk], psb[:, kk, 0:D]).then_inc(s_w0c, 1)

                def norm(i, u):
                    t = 2 * i + u
                    rest(k, v, s_x[u], 16 * (i + 1))
                    rest(k, v, s_tp, t + 1)
                    ln.rows(v, t, xt[:, u], xn[:, u])
                    v.sem_inc(s_xn, 1)

                def out(i, u):
                    t = 2 * i + u
                    rest(k, v, s_h[u], 16 * (i + 1))
                    for c in range(1, NC, 2):
                        rest(k, v, s_mm, (NC + 1) * t + c + 1)
                        v.tensor_copy(hst[:, u, c * 512:(c + 1) * 512], psm[:, c % 4]).then_inc(s_ed, 1)
                    rest(k, v, s_o[u], 16 * (i + 1))
                    rest(k, v, s_mm, (NC + 1) * (t + 1))
                    v.tensor_tensor(bst[:, u], psb[:, u, 0:D], xt[:, u], ALU.add).then_inc(s_b1, 1)
                    rest(k, v, s_b1, t + 1)
                    v.tensor_tensor(bst[:, u], bst[:, u], bias[:], ALU.add).then_inc(s_b, 1)

                v.wait_ge(s_w0, 32)
                norm(0, 0)
                with v.Fori(0, k.NT // 2 - 1) as i:
                    norm(i, 1)
                    out(i, 0)
                    norm(i + 1, 0)
                    out(i, 1)
                last = k.NT // 2 - 1
                norm(last, 1)
                out(last, 0)
                out(last, 1)

            @block.scalar
            def _(act):
                act.sem_inc(s_xt, 2)
                act.sem_inc(s_ea, 2)

                def out(i, u):
                    t = 2 * i + u
                    rest(k, act, s_tp, t + 3)
                    act.copy(xnT[:, u], pst[:, u]).then_inc(s_xt, 1)
                    rest(k, act, s_h[u], 16 * (i + 1))
                    for c in range(0, NC, 2):
                        rest(k, act, s_mm, (NC + 1) * t + c + 1)
                        act.copy(hst[:, u, c * 512:(c + 1) * 512], psm[:, c % 4]).then_inc(s_ea, 1)

                ln.root(act, 0)
                with act.Fori(0, k.NT // 2 - 1) as i:
                    ln.root(act, 2 * i + 1)
                    out(i, 0)
                    ln.root(act, 2 * i + 2)
                    out(i, 1)
                ln.root(act, k.NT - 1)
                out(k.NT // 2 - 1, 0)
                out(k.NT // 2 - 1, 1)

            @block.tensor
            def _(pe):
                pe.sem_inc(s_tp, 2)
                pe.wait_ge(s_w0, 32)
                for kk in range(2):
                    for a in range(2):
                        mm = pe.transpose(psb[:, kk, a * P:(a + 1) * P], w0raw[:, a, kk * P:(kk + 1) * P], k.ident[:])
                    mm.then_inc(s_w0t, 1)
                pe.wait_ge(s_w0c, 2)
                pe.wait_ge(s_w, 16 * R)
                with pe.Fori(0, k.NT // 2) as i:
                    for u in range(2):
                        t = 2 * i + u
                        rest(k, pe, s_xn, t + 1)
                        rest(k, pe, s_xt, t + 1)
                        for kk in range(2):
                            mm = pe.transpose(pst[:, u, kk], xn[:, u, kk * P:(kk + 1) * P], k.ident[:])
                        mm.then_inc(s_tp, 1)
                        rest(k, pe, s_xt, t + 3)
                        for c in range(NC):
                            rest(k, pe, s_ed if c % 2 else s_ea, NC // 2 * t + c // 2 + 1)
                            for kk in range(2):
                                mm = pe.matmul(psm[:, c % 4], xnT[:, u, kk], w[:, kk, c * 512:(c + 1) * 512],
                                               start=(kk == 0), stop=(kk == 1))
                            mm.then_inc(s_mm, 1)
                        rest(k, pe, s_b, t + 1)
                        for kk in range(2):
                            mm = pe.matmul(psb[:, u, 0:D], xnT[:, u, kk], w0[:, kk],
                                           start=(kk == 0), stop=(kk == 1))
                        mm.then_inc(s_mm, 1)

            @block.gpsimd
            def _(pool):
                prime(k, pool, s_h + s_o)
                with pool.Fori(0, k.NT // 2) as i:
                    for u in range(2):
                        t = 2 * i + u
                        hold(k, pool, s_ea, NC // 2 * (t + 1) + 2)
                        hold(k, pool, s_ed, NC // 2 * (t + 1) + 2)
                        pool.dma_start(k.hrel[bass.ds(t * P, P)], hst[:, u]).then_inc(s_h[u], 16)
                        hold(k, pool, s_b, t + 3)
                        pool.dma_start(k.x1[bass.ds(t * P, P)], bst[:, u]).then_inc(s_o[u], 16)
                for s in s_h + s_o:
                    pool.wait_ge(s, 16 * (k.NT // 2 + 1))


def stage_gather(k, name, table, rows, weighted):
    nc, D, NG = k.nc, k.D, k.NG
    s_i, s_p, s_mm, s_add, s_wt, s_th, s_t0, s_t1 = (
        k.sem(name + n) for n in ("i", "p", "mm", "add", "wt", "th", "t0", "t1"))
    s_t = (s_t0, s_t1)
    s_m = [[k.pool_dma_sem(f"{name}m{u}{j}") for j in range(PER)] for u in range(2)]
    sems = [s_i, s_p, s_mm, s_add, s_wt, s_th, s_t0, s_t1, *s_m[0], *s_m[1]]
    with ExitStack() as st:
        sb = lambda n, s, d: st.enter_context(nc.sbuf_tensor(name + n, s, d))
        idx = sb("idx", [P, 2, PER], I32)
        msg = sb("msg", [P, 2, PER, D], F32)
        hit = sb("hit", [P, 2, PER, WIN], F32)
        typ = sb("typ", [k.R, 2, EG], I32)
        hotT = sb("hotT", [k.R, 2, EG], F32)
        ps = st.enter_context(nc.psum_tensor(name + "ps", [P, 2, 2, 256], F32))
        psw = st.enter_context(nc.psum_tensor(name + "psw", [P, 2, 512], F32))

        def run(fixed):
            with nc.Block() as block:
                @block.gpsimd
                def _(pool):
                    with pool.Fori(0, NG // 2) as i:
                        for u in range(2):
                            g = 2 * i + u
                            hold(k, pool, s_mm, g + 1)
                            pool.tensor_copy(idx[:, u], rows[:, bass.ds(g, 1), :].rearrange("p o j -> p (o j)")
                                             ).then_inc(s_i, 1)
                            hold(k, pool, s_i, g + 1)
                            for j in range(PER):
                                pool.indirect_dma_start(
                                    msg[:, u, j], None, table,
                                    bass.IndirectOffsetOnAxis(ap=idx[:, u, j:j + 1].bitcast(U32), axis=0)
                                ).then_inc(s_m[u][j], 16)
                    for s in s_m[0] + s_m[1]:
                        pool.wait_ge(s, 16 * (NG // 2))

                if weighted:
                    @block.sync
                    def _(sp):
                        with sp.Fori(0, NG // 2) as i:
                            for u in range(2):
                                g = 2 * i + u
                                rest(k, sp, s_th, g + 1)
                                sp.dma_start(typ[:, u],
                                             k.typ[bass.ds(g * EG, EG)].partition_broadcast(k.R)
                                             ).then_inc(s_t[u], 16)

                @block.vector
                def _(v):
                    v.sem_inc(s_add, 2)
                    v.sem_inc(s_th, 2)

                    def hot(i, u):
                        g = 2 * i + u
                        rest(k, v, s_wt, g + 1)
                        rest(k, v, s_t[u], 16 * (i + 1))
                        v.tensor_scalar(hotT[:, u], typ[:, u], k.part[0:k.R, 0:1], None,
                                        ALU.is_equal).then_inc(s_th, 1)

                    def build(i, u):
                        g = 2 * i + u
                        if weighted:
                            rest(k, v, s_wt, g + 3)
                        rest(k, v, s_mm, g + 1)
                        if weighted:
                            for j in range(PER):
                                ins = v.scalar_tensor_tensor(
                                    out=hit[:, u, j], in0=k.iota[:],
                                    scalar=k.rel[:, bass.ds(g, 1), j:j + 1].rearrange("p o j -> p (o j)"),
                                    in1=psw[:, u, j * P:(j + 1) * P], op0=ALU.is_equal, op1=ALU.mult)
                        else:
                            ins = v.tensor_tensor(
                                hit[:, u], k.iota[:].rearrange("p (o w) -> p o w", o=1).broadcast_to([P, PER, WIN]),
                                k.rel[:, bass.ds(g, 1), :].rearrange("p o (j q) -> p (o j) q", q=1)
                                .broadcast_to([P, PER, WIN]), ALU.is_equal)
                        ins.then_inc(s_p, 1)

                    def add(g, u):
                        at = (v.value_load(k.base[0:1, bass.ds(g, 1)], min_val=0, max_val=k.NP - WIN)
                              if fixed is None else fixed)
                        v.wait_ge(s_mm, g + 3)
                        v.wait_ge(s_add, g + 2)
                        v.tensor_tensor(k.accT[:, :, bass.ds(at, WIN)], k.accT[:, :, bass.ds(at, WIN)],
                                        ps[:, u, :, 0:WIN], ALU.add).then_inc(s_add, 1)

                    if weighted:
                        hot(0, 0)
                        hot(0, 1)
                    build(0, 0)
                    with v.Fori(0, NG // 2 - 1) as i:
                        if weighted:
                            hot(i + 1, 0)
                        build(i, 1)
                        add(2 * i, 0)
                        if weighted:
                            hot(i + 1, 1)
                        build(i + 1, 0)
                        add(2 * i + 1, 1)
                    build(NG // 2 - 1, 1)
                    add(NG - 2, 0)
                    add(NG - 1, 1)
                    v.wait_ge(s_add, NG + 2)

                @block.tensor
                def _(pe):
                    pe.sem_inc(s_mm, 2)
                    pe.sem_inc(s_wt, 2)

                    def weigh(g, u):
                        at = (pe.value_load(k.base[0:1, bass.ds(g, 1)], min_val=0, max_val=k.NP - WIN)
                              if fixed is None else fixed)
                        hold(k, pe, s_th, g + 3)
                        for j in range(PER):
                            mm = pe.matmul(psw[:, u, j * P:(j + 1) * P], hotT[:, u, j * P:(j + 1) * P],
                                           k.degT[:, bass.ds(at, WIN)], start=True, stop=True)
                        mm.then_inc(s_wt, 1)

                    def sums(i, u):
                        g = 2 * i + u
                        rest(k, pe, s_p, g + 1)
                        rest(k, pe, s_add, g + 1)
                        for j in range(PER):
                            rest(k, pe, s_m[u][j], 16 * (i + 1))
                        for kk in range(2):
                            for j in range(PER):
                                mm = pe.matmul(ps[:, u, kk, 0:WIN], msg[:, u, j, kk * P:(kk + 1) * P],
                                               hit[:, u, j], start=(j == 0), stop=(j == PER - 1))
                        mm.then_inc(s_mm, 1)

                    if weighted:
                        weigh(0, 0)
                    with pe.Fori(0, NG // 2 - 1) as i:
                        if weighted:
                            weigh(2 * i + 1, 1)
                        sums(i, 0)
                        if weighted:
                            weigh(2 * i + 2, 0)
                        sums(i, 1)
                    if weighted:
                        weigh(NG - 1, 1)
                    sums(NG // 2 - 1, 0)
                    sums(NG // 2 - 1, 1)
            clear(k, sems)

        with nc.Block() as block:
            @block.vector
            def _(v):
                link = Chain(v, k.sem(name + "z"))
                link(v.memset(k.accT[:], 0.0))
                link(v.memset(k.win_f[:], 0.0))
        for_windows(k, name, run)


def stage_route(k, gate_w, gate_b):
    nc, D, NT, EX = k.nc, k.D, k.NT, k.EX
    (s_cs, s_cx, s_ld, s_x0, s_x1, s_tp, s_add, s_ln, s_xn, s_t2, s_xt, s_lg, s_lc, s_st, s_o0, s_o1, s_rt, s_ex, s_pe) = (
        (k.pool_dma_sem if n in ("o0", "o1") else k.sem)("g_" + n) for n in ("cs", "cx", "ld", "x0", "x1", "tp", "add", "ln", "xn", "t2", "xt", "lg", "lc", "st",
                                  "o0", "o1", "rt", "ex", "pe"))
    s_x, s_o = (s_x0, s_x1), (s_o0, s_o1)
    with ExitStack() as st:
        sb = lambda n, s, d=F32: st.enter_context(nc.sbuf_tensor("g_" + n, s, d))
        ps_ = lambda n, s: st.enter_context(nc.psum_tensor("g_" + n, s, F32))
        xn = sb("xn", [P, NT, D])
        xs = sb("xs", [P, 2, D])
        stg = sb("stg", [P, 2, 2, P])
        gw = sb("gw", [P, 2, EX])
        gb = sb("gb", [P, EX])
        xb = sb("xb", [P, 2, D])
        xo = sb("xo", [P, 2, D])
        ln = LayerNorm(k, sb)
        xnT = sb("xnT", [P, 2, 2, P])
        lg = sb("lg", [P, NT, EX])
        psa = ps_("psa", [P, 2, 2, 256])
        pst = ps_("pst", [P, 2, 2, 256])
        psl = ps_("psl", [P, 2, 512])
        with nc.Block() as block:
            @block.sync
            def _(sp):
                sp.dma_start(gw[:], gate_w.rearrange("(k p) e -> p k e", p=P)).then_inc(s_ld, 16)
                sp.dma_start(gb[:], gate_b.partition_broadcast(P)).then_inc(s_ld, 16)
                with sp.Fori(0, NT // 2) as i:
                    for u in range(2):
                        rest(k, sp, s_add, 2 * i + u + 1)
                        sp.dma_start(xb[:, u], k.x1[bass.ds((2 * i + u) * P, P)]).then_inc(s_x[u], 16)

            @block.tensor
            def _(pe):
                pe.sem_inc(s_t2, 2)
                pe.wait_ge(s_ld, 32)
                with pe.Fori(0, NT // 2) as i:
                    for u in range(2):
                        t = 2 * i + u
                        rest(k, pe, s_cs, t + 1)
                        rest(k, pe, s_add, t + 1)
                        for kk in range(2):
                            mm = pe.transpose(psa[:, u].rearrange("p a b -> p (a b)")[:, kk * P:(kk + 1) * P],
                                              stg[:, u, kk], k.ident[:])
                        mm.then_inc(s_tp, 1)
                        rest(k, pe, s_xn, t + 1)
                        rest(k, pe, s_xt, t + 1)
                        for kk in range(2):
                            mm = pe.transpose(pst[:, u, kk, 0:P], xs[:, u, kk * P:(kk + 1) * P], k.ident[:])
                        mm.then_inc(s_t2, 1)
                        rest(k, pe, s_xt, t + 3)
                        rest(k, pe, s_lc, t + 1)
                        for kk in range(2):
                            mm = pe.matmul(psl[:, u, 0:EX], xnT[:, u, kk], gw[:, kk], start=(kk == 0), stop=(kk == 1))
                        mm.then_inc(s_lg, 1)

            @block.scalar
            def _(act):
                act.sem_inc(s_xt, 2)
                act.sem_inc(s_cx, 2)

                def stage(t, u):
                    if not isinstance(t, int) or t:
                        hold(k, act, s_tp, t)
                    act.copy(stg[:, u], k.accT[:, :, bass.ds(t * P, P)]).then_inc(s_cs, 1)

                def back(t, u):
                    ln.root(act, t)
                    hold(k, act, s_xn, t + 1)
                    act.copy(xn[:, bass.ds(t, 1), :].rearrange("p o d -> p (o d)"), xs[:, u]).then_inc(s_cx, 1)
                    rest(k, act, s_t2, t + 3)
                    act.copy(xnT[:, u], pst[:, u, :, 0:P]).then_inc(s_xt, 1)

                stage(0, 0)
                with act.Fori(0, NT // 2 - 1) as i:
                    stage(2 * i + 1, 1)
                    back(2 * i, 0)
                    stage(2 * i + 2, 0)
                    back(2 * i + 1, 1)
                stage(NT - 1, 1)
                back(NT - 2, 0)
                back(NT - 1, 1)

            @block.vector
            def _(v):
                v.sem_inc(s_add, 2)
                v.sem_inc(s_lc, 2)
                v.wait_ge(s_ld, 32)
                with v.Fori(0, NT // 2) as i:
                    for u in range(2):
                        t = 2 * i + u
                        rest(k, v, s_x[u], 16 * (i + 1))
                        rest(k, v, s_tp, t + 1)
                        rest(k, v, s_o[u], 16 * (i + 1))
                        v.tensor_tensor(xo[:, u], psa[:, u].rearrange("p a b -> p (a b)")[:, 0:D],
                                        xb[:, u], ALU.add).then_inc(s_add, 1)
                        rest(k, v, s_add, t + 3)
                        rest(k, v, s_cx, t + 1)
                        rest(k, v, s_t2, t + 1)
                        ln.rows(v, t, xo[:, u], xs[:, u])
                        v.sem_inc(s_xn, 1)
                        rest(k, v, s_lg, t + 1)
                        v.tensor_tensor(lg[:, bass.ds(t, 1), :].rearrange("p o e -> p (o e)"),
                                        psl[:, u, 0:EX], gb[:], ALU.add).then_inc(s_lc, 1)

            @block.gpsimd
            def _(pool):
                prime(k, pool, s_o)
                with pool.Fori(0, NT // 2) as i:
                    for u in range(2):
                        t = 2 * i + u
                        hold(k, pool, s_add, t + 3)
                        pool.dma_start(k.x1[bass.ds(t * P, P)], xo[:, u]).then_inc(s_o[u], 16)
                for s in s_o:
                    pool.wait_ge(s, 16 * (NT // 2 + 1))

        N8 = NT * EX
        mx, me, se, pick, val = (sb(n, [P, NT]) for n in ("mx", "me", "se", "pick", "val"))
        e_, eq, oh, cum, tot = (sb(n, [P, NT, EX]) for n in ("e", "eq", "oh", "cum", "tot"))
        tot2, jm, tok, kept, slot, t3 = (sb("tot2", [P, NT, EX]), sb("jm", [P, EX]), sb("tok", [P, NT]),
                                         sb("kept", [P, NT]), sb("slot", [P, NT]), sb("t3", [P, NT]))
        tok_i = sb("tok_i", [P, NT], I32)
        over_e = lambda a: a.rearrange("p (t o) -> p t o", o=1).broadcast_to([P, NT, EX])
        over_t = lambda a: a.rearrange("p (o e) -> p o e", o=1).broadcast_to([P, NT, EX])
        with nc.Block() as block:
            @block.gpsimd
            def _(pool):
                pool.iota(tok_i[:], pattern=[[P, NT]], base=EX * k.CS, channel_multiplier=1).then_inc(s_st, 1)
                pool.wait_ge(s_st, 1)
                pool.tensor_copy(tok[:], tok_i[:]).then_inc(s_st, 1)
                pool.wait_ge(s_st, 2)

            @block.scalar
            def _(act):
                act.wait_ge(s_rt, 2)
                act.activation(e_[:], e_[:], ACT.Exp).then_inc(s_ex, 1)

            @block.tensor
            def _(pe):
                pe.wait_ge(s_rt, 9)
                pe.matmul(psl[:, 0, 0:N8], k.upper[:], oh[:].rearrange("p t e -> p (t e)"), start=True, stop=True)
                pe.matmul(psl[:, 1, 0:N8], k.ones[:], oh[:].rearrange("p t e -> p (t e)"),
                          start=True, stop=True).then_inc(s_pe, 1)

            @block.vector
            def _(v):
                link = Chain(v, s_rt)
                link(v.tensor_reduce(mx[:], lg[:], AX, ALU.max))
                link(v.tensor_tensor(e_[:], lg[:], over_e(mx[:]), ALU.subtract))
                v.wait_ge(s_ex, 1)
                link(v.tensor_reduce(se[:], e_[:], AX, ALU.add))
                link(v.tensor_reduce(me[:], e_[:], AX, ALU.max))
                link(v.tensor_tensor(eq[:], e_[:], over_e(me[:]), ALU.is_equal))
                link(v.tensor_scalar(jm[:], k.iota[:, 0:EX], float(EX), None, ALU.subtract))
                link(v.tensor_tensor(eq[:], eq[:], over_t(jm[:]), ALU.mult))
                link(v.tensor_reduce(pick[:], eq[:], AX, ALU.min))
                link(v.tensor_tensor(oh[:], over_t(jm[:]), over_e(pick[:]), ALU.is_equal))
                v.wait_ge(s_pe, 1)
                link(v.memset(tot[:, 0:1], 0.0))
                link(v.tensor_copy(tot[:, 1:NT], psl[:, 1, 0:N8].rearrange("p (t e) -> p t e", e=EX)[:, 0:NT - 1]))
                a, b, n = tot, tot2, 1
                while n < NT:
                    link(v.tensor_copy(b[:, 0:n], a[:, 0:n]))
                    link(v.tensor_tensor(b[:, n:NT], a[:, n:NT], a[:, 0:NT - n], ALU.add))
                    a, b, n = b, a, 2 * n
                link(v.tensor_tensor(cum[:], psl[:, 0, 0:N8].rearrange("p (t e) -> p t e", e=EX), a[:], ALU.add))
                link(v.tensor_tensor(cum[:], cum[:], oh[:], ALU.mult))
                link(v.tensor_reduce(val[:], cum[:], AX, ALU.add))
                link(v.tensor_scalar(kept[:], val[:], float(k.CAP), None, ALU.is_le))
                link(v.reciprocal(se[:], se[:]))
                link(v.tensor_tensor(me[:], me[:], se[:], ALU.mult))
                link(v.tensor_tensor(k.gate[:], me[:], kept[:], ALU.mult))
                link(v.tensor_scalar(pick[:], pick[:], float(EX), float(k.CS), ALU.add, ALU.mult))
                link(v.tensor_scalar(t3[:], val[:], float(k.CAP), -1.0, ALU.min, ALU.add))
                link(v.tensor_tensor(slot[:], pick[:], t3[:], ALU.add))
                link(v.tensor_copy(k.slot_read[:], slot[:]))
                v.wait_ge(s_st, 2)
                link(v.tensor_tensor(slot[:], slot[:], tok[:], ALU.subtract))
                link(v.tensor_tensor(slot[:], slot[:], kept[:], ALU.mult))
                link(v.tensor_tensor(slot[:], slot[:], tok[:], ALU.add))
                link(v.tensor_copy(k.slot_write[:], slot[:]))

        s_i, s_s = k.sem("g_i"), (k.pool_dma_sem("g_s0"), k.pool_dma_sem("g_s1"))
        with nc.Block() as block:
            @block.gpsimd
            def _(pool):
                prime(k, pool, s_s)
                with pool.Fori(0, NT // 2) as i:
                    for u in range(2):
                        t = 2 * i + u
                        hold(k, pool, s_s[u], 16 * (i + 1))
                        pool.tensor_copy(k.islot[:, u:u + 1], k.slot_write[:, bass.ds(t, 1)]).then_inc(s_i, 1)
                        pool.tensor_copy(xb[:, u], xn[:, bass.ds(t, 1), :].rearrange("p o d -> p (o d)")
                                         ).then_inc(s_i, 1)
                        hold(k, pool, s_i, 2 * t + 2)
                        pool.indirect_dma_start(
                            k.buf, bass.IndirectOffsetOnAxis(ap=k.islot[:, u:u + 1].bitcast(U32), axis=0),
                            xb[:, u], None).then_inc(s_s[u], 16)
                for s in s_s:
                    pool.wait_ge(s, 16 * (NT // 2 + 1))


def stage_experts(k, w1, b1, w2, b2):
    nc, D, EX, CS = k.nc, k.D, k.EX, k.CS
    F = w1.shape[2]
    FB, TB = F // P, CS // P
    nm = ("b", "bt", "bc", "w0", "w1", "v0", "v1", "x0", "x1", "c0", "c1", "tp", "tc", "h", "hc", "y", "yc", "sc")
    S = {n: (k.pool_dma_sem if n == "sc" else k.sem)("x_" + n) for n in nm}
    s_w, s_v, s_x, s_c = ((S[a + "0"], S[a + "1"]) for a in ("w", "v", "x", "c"))
    with ExitStack() as st:
        sb = lambda n, s, d=F32: st.enter_context(nc.sbuf_tensor("x_" + n, s, d))
        ps_ = lambda n, s: st.enter_context(nc.psum_tensor("x_" + n, s, F32))
        b1r, b1T = sb("b1r", [EX * FB, P]), sb("b1T", [P, EX, FB])
        w1s, w2s = sb("w1s", [P, 2, 2, F]), sb("w2s", [P, 2, FB, D])
        b2s = sb("b2s", [P, 2, D])
        xr = sb("xr", [P, 2, TB, D])
        xT = sb("xT", [P, 2, CS])
        hT = sb("hT", [P, FB, CS])
        ys = sb("ys", [P, TB, D])
        pst, psh, psy = ps_("pst", [P, 2, 512]), ps_("psh", [P, 4, 512]), ps_("psy", [P, 2, 512])
        HB = CS // 512
        with nc.Block() as block:
            @block.sync
            def _(sp):
                sp.dma_start(b1r[:], b1.rearrange("e (f p) -> (e f) p", p=P)).then_inc(S["b"], 16)
                with sp.Fori(0, EX // 2) as i:
                    for u in range(2):
                        e = 2 * i + u
                        rest(k, sp, S["yc"], TB * e + TB)
                        one = lambda a: a[bass.ds(e, 1)]
                        sp.dma_start(xr[:, u], k.buf[bass.ds(e * CS, CS)].rearrange("(a p) d -> p a d", p=P)).then_inc(s_x[u], 16)
                        sp.dma_start(w1s[:, u], one(w1).rearrange("o (k p) f -> p (o k) f", p=P)).then_inc(s_w[u], 16)
                        sp.dma_start(w2s[:, u], one(w2).rearrange("o (f p) d -> p (o f) d", p=P)).then_inc(s_v[u], 16)
                        sp.dma_start(b2s[:, u], one(b2).rearrange("o d -> (o d)").partition_broadcast(P)).then_inc(s_c[u], 16)

            @block.tensor
            def _(pe):
                pe.wait_ge(S["b"], 16)
                pe.transpose(pst[:, 0, 0:EX * FB], b1r[:], k.ident[0:EX * FB, 0:EX * FB]).then_inc(S["bt"], 1)
                pe.wait_ge(S["bc"], 1)
                pe.sem_inc(S["y"], 1)
                pe.sem_inc(S["h"], 1)
                with pe.Fori(0, EX // 2) as i:
                    for u in range(2):
                        e = 2 * i + u
                        rest(k, pe, s_x[u], 16 * (i + 1))
                        for n in range(TB):
                            rest(k, pe, S["tc"], TB * e + n + 1)
                            for kk in range(2):
                                mm = pe.transpose(pst[:, n % 2, kk * P:(kk + 1) * P], xr[:, u, n, kk * P:(kk + 1) * P],
                                                  k.ident[:])
                            mm.then_inc(S["tp"], 1)
                        rest(k, pe, S["tc"], TB * (e + 1) + 2)
                        rest(k, pe, s_w[u], 16 * (i + 1))
                        for f in range(FB):
                            for h in range(HB):
                                n = f * HB + h
                                rest(k, pe, S["hc"], FB * HB * e + n + 1)
                                for kk in range(2):
                                    mm = pe.matmul(psh[:, n % 4], w1s[:, u, kk, f * P:(f + 1) * P],
                                                   xT[:, kk, h * 512:(h + 1) * 512], start=(kk == 0), stop=(kk == 1))
                                mm.then_inc(S["h"], 1)
                        rest(k, pe, S["hc"], FB * HB * (e + 1) + 4)
                        rest(k, pe, s_v[u], 16 * (i + 1))
                        for n in range(TB):
                            rest(k, pe, S["yc"], TB * e + n + 2 * TB - 1)
                            for f in range(FB):
                                mm = pe.matmul(psy[:, n % 2, 0:D], hT[:, f, n * P:(n + 1) * P], w2s[:, u, f],
                                               start=(f == 0), stop=(f == FB - 1))
                            mm.then_inc(S["y"], 1)

            @block.scalar
            def _(act):
                act.sem_inc(S["hc"], 4)
                act.wait_ge(S["bt"], 1)
                act.copy(b1T[:].rearrange("p e f -> p (e f)"), pst[:, 0, 0:EX * FB]).then_inc(S["bc"], 1)
                act.wait_ge(S["bc"], 1)
                with act.Fori(0, EX // 2) as i:
                    for u in range(2):
                        e = 2 * i + u
                        rest(k, act, S["y"], TB * e + 1)
                        for n in range(FB * HB):
                            f, h = n // HB, n % HB
                            hold(k, act, S["h"], FB * HB * e + n + 2)
                            act.activation(hT[:, f, h * 512:(h + 1) * 512], psh[:, n % 4], ACT.Relu,
                                           bias=b1T[:, bass.ds(e, 1), f:f + 1].rearrange("p o f -> p (o f)")
                                           ).then_inc(S["hc"], 1)

            @block.vector
            def _(v):
                v.sem_inc(S["tc"], 2)
                v.sem_inc(S["yc"], 2 * TB)
                with v.Fori(0, EX // 2) as i:
                    for u in range(2):
                        e = 2 * i + u
                        for n in range(TB):
                            rest(k, v, S["tp"], TB * e + n + 1)
                            if n == 0:
                                rest(k, v, S["h"], FB * HB * e + 1)
                            v.tensor_copy(xT[:, :, n * P:(n + 1) * P],
                                          pst[:, n % 2, 0:2 * P].rearrange("p (k t) -> p k t", k=2)).then_inc(S["tc"], 1)
                        rest(k, v, S["sc"], 16 * (e + 1))
                        rest(k, v, s_c[u], 16 * (i + 1))
                        for n in range(TB):
                            rest(k, v, S["y"], TB * e + n + 2)
                            v.tensor_tensor(ys[:, n], psy[:, n % 2, 0:D], b2s[:, u], ALU.add).then_inc(S["yc"], 1)

            @block.gpsimd
            def _(pool):
                prime(k, pool, (S["sc"],))
                with pool.Fori(0, EX // 2) as i:
                    for u in range(2):
                        e = 2 * i + u
                        hold(k, pool, S["yc"], TB * (e + 1) + 2 * TB)
                        pool.dma_start(k.ybuf[bass.ds(e * CS, CS)].rearrange("(a p) d -> p a d", p=P), ys[:]).then_inc(S["sc"], 16)
                pool.wait_ge(S["sc"], 16 * (EX + 1))


def stage_combine(k, W):
    nc, D, NT = k.nc, k.D, k.NT
    nm = ("w", "x0", "x1", "i", "y0", "y1", "m", "g", "a", "ln", "xn", "tp", "xt", "mm", "ev", "o0", "o1", "q0", "q1")
    S = {n: (k.pool_dma_sem if n in ("y0", "y1", "o0", "o1", "q0", "q1") else k.sem)("c_" + n) for n in nm}
    s_x, s_y, s_o, s_q = ((S[a + "0"], S[a + "1"]) for a in ("x", "y", "o", "q"))
    with ExitStack() as st:
        sb = lambda n, s, d=F32: st.enter_context(nc.sbuf_tensor("c_" + n, s, d))
        ps_ = lambda n, s: st.enter_context(nc.psum_tensor("c_" + n, s, F32))
        w = sb("w", [P, 2, D])
        big, small, none = sb("big", [P, D]), sb("small", [P, D]), sb("none", [P, D])
        xb, yr, xo = sb("xb", [P, 2, D]), sb("yr", [P, 2, D]), sb("xo", [P, 2, D])
        m1, m2, m3 = (sb(n, [P, D], U8) for n in ("m1", "m2", "m3"))
        ln = LayerNorm(k, sb)
        xn, xnT, gs = sb("xn", [P, 2, D]), sb("xnT", [P, 2, 2, P]), sb("gs", [P, 2, D])
        pst, psm = ps_("pst", [P, 2, 512]), ps_("psm", [P, 2, 512])
        G = 6
        with nc.Block() as block:
            @block.sync
            def _(sp):
                sp.dma_start(w[:], W.rearrange("(k p) o -> p k o", p=P)).then_inc(S["w"], 16)
                with sp.Fori(0, NT // 2) as i:
                    for u in range(2):
                        t = 2 * i + u
                        rest(k, sp, S["a"], t + 1)
                        sp.dma_start(xb[:, u], k.x1[bass.ds(t * P, P)]).then_inc(s_x[u], 16)

            @block.gpsimd
            def _(pool):
                link = Chain(pool, S["m"])
                link(pool.memset(big[:], 10000.0))
                link(pool.memset(small[:], -10000.0))
                link(pool.memset(none[:], 0.0))
                prime(k, pool, s_o + s_q)

                def gather(i, u):
                    t = 2 * i + u
                    hold(k, pool, S["a"], t + 1)
                    pool.tensor_copy(k.islot[:, u:u + 1], k.slot_read[:, bass.ds(t, 1)]).then_inc(S["i"], 1)
                    hold(k, pool, S["i"], t + 1)
                    pool.indirect_dma_start(yr[:, u], None, k.ybuf,
                                            bass.IndirectOffsetOnAxis(ap=k.islot[:, u:u + 1].bitcast(U32), axis=0)
                                            ).then_inc(s_y[u], 16)

                def out(i, u):
                    t = 2 * i + u
                    hold(k, pool, S["a"], t + 3)
                    pool.dma_start(k.x2[bass.ds(t * P, P)], xo[:, u]).then_inc(s_o[u], 16)
                    hold(k, pool, S["ev"], t + 3)
                    pool.dma_start(k.gtab[bass.ds(t * P, P)], gs[:, u]).then_inc(s_q[u], 16)

                gather(0, 0)
                with pool.Fori(0, NT // 2 - 1) as i:
                    gather(i, 1)
                    out(i, 0)
                    gather(i + 1, 0)
                    out(i, 1)
                last = NT // 2 - 1
                gather(last, 1)
                out(last, 0)
                out(last, 1)
                for s in s_o + s_q:
                    pool.wait_ge(s, 16 * (NT // 2 + 1))

            @block.vector
            def _(v):
                v.sem_inc(S["a"], 2)
                v.wait_ge(S["m"], 3)
                with v.Fori(0, NT // 2) as i:
                    for u in range(2):
                        t = 2 * i + u
                        y = yr[:, u]
                        rest(k, v, s_y[u], 16 * (i + 1))
                        link = Chain(v, S["g"], k, t * G, hold)
                        link(v.tensor_scalar(y, y, k.gate[:, bass.ds(t, 1)], None, ALU.mult))
                        v.tensor_scalar(m1[:], y, float("inf"), None, ALU.is_equal)
                        v.tensor_scalar(m2[:], y, float("-inf"), None, ALU.is_equal)
                        link(v.tensor_tensor(m3[:], y, y, ALU.not_equal))
                        link(v.copy_predicated(y, m1[:], big[:]))
                        link(v.copy_predicated(y, m2[:], small[:]))
                        link(v.copy_predicated(y, m3[:], none[:]))
                        rest(k, v, s_x[u], 16 * (i + 1))
                        rest(k, v, s_o[u], 16 * (i + 1))
                        link(v.tensor_tensor(xo[:, u], xb[:, u], y, ALU.add))
                        v.sem_inc(S["a"], 1)
                        rest(k, v, S["tp"], t + 1)
                        ln.rows(v, t, xo[:, u], xn[:, u])
                        v.sem_inc(S["xn"], 1)

            @block.scalar
            def _(act):
                act.sem_inc(S["xt"], 2)
                act.sem_inc(S["ev"], 2)
                with act.Fori(0, NT // 2) as i:
                    for u in range(2):
                        t = 2 * i + u
                        ln.root(act, t)
                        rest(k, act, S["tp"], t + 3)
                        act.copy(xnT[:, u].rearrange("p k t -> p (k t)"), pst[:, u, 0:2 * P]).then_inc(S["xt"], 1)
                        rest(k, act, S["mm"], t + 1)
                        hold(k, act, s_q[u], 16 * (i + 1))
                        act.activation(gs[:, u], psm[:, u, 0:D], ACT.Copy, scale=k.dinv[:, bass.ds(t, 1)]
                                       ).then_inc(S["ev"], 1)

            @block.tensor
            def _(pe):
                pe.sem_inc(S["tp"], 2)
                pe.wait_ge(S["w"], 16)
                with pe.Fori(0, NT // 2) as i:
                    for u in range(2):
                        t = 2 * i + u
                        rest(k, pe, S["xn"], t + 1)
                        rest(k, pe, S["xt"], t + 1)
                        for kk in range(2):
                            mm = pe.transpose(pst[:, u, kk * P:(kk + 1) * P], xn[:, u, kk * P:(kk + 1) * P], k.ident[:])
                        mm.then_inc(S["tp"], 1)
                        rest(k, pe, S["xt"], t + 3)
                        rest(k, pe, S["ev"], t + 1)
                        for kk in range(2):
                            mm = pe.matmul(psm[:, u, 0:D], xnT[:, u, kk], w[:, kk], start=(kk == 0), stop=(kk == 1))
                        mm.then_inc(S["mm"], 1)


def stage_x3(k, b):
    nc, D, NT = k.nc, k.D, k.NT
    nm = ("cs", "b", "x0", "x1", "z0", "z1", "tp", "a", "q", "ln", "xn", "t2", "xt", "o0", "o1")
    S = {n: (k.pool_dma_sem if n in ("o0", "o1") else k.sem)("n_" + n) for n in nm}
    s_x, s_z, s_o = ((S[a + "0"], S[a + "1"]) for a in ("x", "z", "o"))
    with ExitStack() as st:
        sb = lambda n, s, d=F32: st.enter_context(nc.sbuf_tensor("n_" + n, s, d))
        ps_ = lambda n, s: st.enter_context(nc.psum_tensor("n_" + n, s, F32))
        bs = sb("bs", [P, D])
        xb, gb, xo, xn = (sb(n, [P, 2, D]) for n in ("xb", "gb", "xo", "xn"))
        stg = sb("stg", [P, 2, 2, P])
        z, z2 = sb("z", [P, D]), sb("z2", [P, D])
        ln = LayerNorm(k, sb)
        psa, pst = ps_("psa", [P, 2, 512]), ps_("pst", [P, 2, 512])
        Q = 4
        with nc.Block() as block:
            @block.sync
            def _(sp):
                sp.dma_start(bs[:], b.partition_broadcast(P)).then_inc(S["b"], 16)
                with sp.Fori(0, NT // 2) as i:
                    for u in range(2):
                        t = 2 * i + u
                        rest(k, sp, S["a"], t + 1)
                        sp.dma_start(xb[:, u], k.x2[bass.ds(t * P, P)]).then_inc(s_x[u], 16)
                        sp.dma_start(gb[:, u], k.gtab[bass.ds(t * P, P)]).then_inc(s_z[u], 16)

            @block.gpsimd
            def _(pool):
                prime(k, pool, s_o)
                with pool.Fori(0, NT // 2) as i:
                    for u in range(2):
                        t = 2 * i + u
                        hold(k, pool, S["a"], t + 3)
                        pool.dma_start(k.x3[bass.ds(t * P, P)], xo[:, u]).then_inc(s_o[u], 16)
                for s in s_o:
                    pool.wait_ge(s, 16 * (NT // 2 + 1))

            @block.tensor
            def _(pe):
                pe.sem_inc(S["t2"], 2)

                def sums(i, u):
                    t = 2 * i + u
                    rest(k, pe, S["cs"], t + 1)
                    rest(k, pe, S["a"], t + 1)
                    for kk in range(2):
                        mm = pe.transpose(psa[:, u, kk * P:(kk + 1) * P], stg[:, u, kk], k.ident[:])
                    mm.then_inc(S["tp"], 1)

                def back(i, u):
                    t = 2 * i + u
                    rest(k, pe, S["xn"], t + 1)
                    rest(k, pe, S["xt"], t + 1)
                    for kk in range(2):
                        mm = pe.transpose(pst[:, u, kk * P:(kk + 1) * P], xn[:, u, kk * P:(kk + 1) * P], k.ident[:])
                    mm.then_inc(S["t2"], 1)

                sums(0, 0)
                with pe.Fori(0, NT // 2 - 1) as i:
                    sums(i, 1)
                    back(i, 0)
                    sums(i + 1, 0)
                    back(i, 1)
                sums(NT // 2 - 1, 1)
                back(NT // 2 - 1, 0)
                back(NT // 2 - 1, 1)

            @block.scalar
            def _(act):
                act.sem_inc(S["xt"], 2)

                def stage(t, u):
                    if not isinstance(t, int) or t:
                        hold(k, act, S["tp"], t)
                    act.copy(stg[:, u], k.accT[:, :, bass.ds(t * P, P)]).then_inc(S["cs"], 1)

                def back(t, u):
                    ln.root(act, t)
                    hold(k, act, S["t2"], t + 3)
                    act.copy(k.accT[:, :, bass.ds(t * P, P)],
                             pst[:, u, 0:2 * P].rearrange("p (k t) -> p k t", k=2)).then_inc(S["xt"], 1)

                stage(0, 0)
                with act.Fori(0, NT // 2 - 1) as i:
                    stage(2 * i + 1, 1)
                    back(2 * i, 0)
                    stage(2 * i + 2, 0)
                    back(2 * i + 1, 1)
                stage(NT - 1, 1)
                back(NT - 2, 0)
                back(NT - 1, 1)

            @block.vector
            def _(v):
                v.sem_inc(S["a"], 2)
                v.wait_ge(S["b"], 16)
                with v.Fori(0, NT // 2) as i:
                    for u in range(2):
                        t = 2 * i + u
                        rest(k, v, S["tp"], t + 1)
                        rest(k, v, s_x[u], 16 * (i + 1))
                        rest(k, v, s_z[u], 16 * (i + 1))
                        link = Chain(v, S["q"], k, t * Q)
                        link(v.tensor_tensor(z[:], psa[:, u, 0:D], gb[:, u], ALU.add))
                        link(v.scalar_tensor_tensor(out=z[:], in0=z[:], scalar=k.dinv[:, bass.ds(t, 1)], in1=bs[:],
                                                    op0=ALU.mult, op1=ALU.add))
                        link(v.scalar_tensor_tensor(out=z2[:], in0=z[:], scalar=0.2, in1=z[:],
                                                    op0=ALU.mult, op1=ALU.max))
                        rest(k, v, s_o[u], 16 * (i + 1))
                        link(v.tensor_tensor(xo[:, u], xb[:, u], z2[:], ALU.add))
                        v.sem_inc(S["a"], 1)
                        rest(k, v, S["t2"], t + 1)
                        ln.rows(v, t, xo[:, u], xn[:, u])
                        v.sem_inc(S["xn"], 1)


GATES = (0, 1, 2, 3, 6, 7, 4, 5)


def stage_inputs(k, W_ih, b_ih, b_hh):
    nc, C, L = k.nc, k.C, k.L
    nm = ("w", "b", "wt", "wc", "mm", "ea", "ed", "o0", "o1", "bs")
    S = {n: k.sem("i_" + n) for n in nm}
    s_o = (S["o0"], S["o1"])
    with ExitStack() as st:
        sb = lambda n, s, d=F32: st.enter_context(nc.sbuf_tensor("i_" + n, s, d))
        ps_ = lambda n, s: st.enter_context(nc.psum_tensor("i_" + n, s, F32))
        wr = sb("wr", [P, 8, 2 * P])
        wT = sb("wT", [P, 2, 8, P])
        br = sb("br", [16, P])
        bsum = sb("bsum", [P, 8])
        xs = sb("xs", [P, 2, 8, C])
        psw, psm = ps_("psw", [P, 2, 512]), ps_("psm", [P, 4, 512])
        xT = k.accT[:, :, 0:k.N].rearrange("p k (c s) -> p k s c", s=L)
        with nc.Block() as block:
            @block.sync
            def _(sp):
                sp.dma_start(wr[:], W_ih.rearrange("(g p) d -> p g d", p=P)).then_inc(S["w"], 16)
                sp.dma_start(br[0:8], b_ih.rearrange("(g p) -> g p", p=P)).then_inc(S["w"], 16)
                sp.dma_start(br[8:16], b_hh.rearrange("(g p) -> g p", p=P)).then_inc(S["w"], 16)
                prime(k, sp, s_o)
                with sp.Fori(0, L // 2) as i:
                    for u in range(2):
                        s = 2 * i + u
                        rest(k, sp, S["ea"], 4 * s + 8)
                        rest(k, sp, S["ed"], 4 * s + 8)
                        sp.dma_start(k.xp[bass.ds(s, 1)].rearrange("o p g c -> p (o g) c"), xs[:, u]).then_inc(s_o[u], 16)
                for s in s_o:
                    sp.wait_ge(s, 16 * (L // 2 + 1))

            @block.tensor
            def _(pe):
                pe.wait_ge(S["w"], 48)
                for n in range(8):
                    if n >= 2:
                        pe.wait_ge(S["wc"], n - 1)
                    for kk in range(2):
                        mm = pe.transpose(psw[:, n % 2, kk * P:(kk + 1) * P], wr[:, GATES[n], kk * P:(kk + 1) * P], k.ident[:])
                    mm.then_inc(S["wt"], 1)
                pe.wait_ge(S["wc"], 8)
                pe.transpose(psw[:, 0, 0:16], br[:], k.ident[0:16, 0:16]).then_inc(S["wt"], 1)
                pe.wait_ge(S["bs"], 8)
                with pe.Fori(0, L // 2) as i:
                    for u in range(2):
                        s = 2 * i + u
                        for n in range(8):
                            rest(k, pe, S["ed"] if n % 2 else S["ea"], 4 * s + n // 2 + 3)
                            for kk in range(2):
                                mm = pe.matmul(psm[:, n % 4, 0:C], wT[:, kk, n],
                                               xT[:, kk, bass.ds(s, 1), :].rearrange("p o c -> p (o c)"),
                                               start=(kk == 0), stop=(kk == 1))
                            mm.then_inc(S["mm"], 1)

            @block.scalar
            def _(act):
                act.wait_ge(S["bs"], 8)
                act.sem_inc(S["ea"], 4)
                with act.Fori(0, L // 2) as i:
                    for u in range(2):
                        s = 2 * i + u
                        rest(k, act, s_o[u], 16 * (i + 1))
                        for n in range(0, 8, 2):
                            rest(k, act, S["mm"], 8 * s + n + 1)
                            act.activation(xs[:, u, n], psm[:, n % 4, 0:C], ACT.Identity, bias=bsum[:, n:n + 1]
                                           ).then_inc(S["ea"], 1)

            @block.vector
            def _(v):
                for n in range(8):
                    v.wait_ge(S["wt"], n + 1)
                    v.tensor_copy(wT[:, :, n], psw[:, n % 2, 0:2 * P].rearrange("p (k t) -> p k t", k=2)).then_inc(S["wc"], 1)
                v.wait_ge(S["wt"], 9)
                v.tensor_copy(wr[:, 0, 0:8], psw[:, 0, 0:8]).then_inc(S["b"], 1)
                v.wait_ge(S["b"], 1)
                for n in range(8):
                    g = GATES[n]
                    v.tensor_tensor(bsum[:, n:n + 1], psw[:, 0, 8 + g:9 + g], wr[:, 0, g:g + 1], ALU.add).then_inc(S["bs"], 1)
                v.wait_ge(S["bs"], 8)
                v.sem_inc(S["ed"], 4)
                with v.Fori(0, L // 2) as i:
                    for u in range(2):
                        s = 2 * i + u
                        rest(k, v, s_o[u], 16 * (i + 1))
                        for n in range(1, 8, 2):
                            rest(k, v, S["mm"], 8 * s + n + 1)
                            v.tensor_scalar(xs[:, u, n], psm[:, n % 4, 0:C], bsum[:, n:n + 1], None, ALU.add
                                            ).then_inc(S["ed"], 1)


def stage_lstm(k, st, W_hh):
    nc, C, L = k.nc, k.C, k.L
    halves = ((0, (C + 1) // 2), ((C + 1) // 2, C))
    nm = ("w", "wt", "wc", "x0", "x1", "z", "mm0", "mm1", "ga0", "ga1", "sg0", "sg1", "cc0", "cc1", "tc0", "tc1",
          "h0", "h1", "d0", "d1", "e", "q", "pe")
    S = {n: k.sem("l_" + n) for n in nm}
    s_x = (S["x0"], S["x1"])
    sb = lambda n, s, d=F32: st.enter_context(nc.sbuf_tensor("l_" + n, s, d))
    ps_ = lambda n, s: st.enter_context(nc.psum_tensor("l_" + n, s, F32))
    k.hall = sb("hall", [P, L + 1, 2, C])
    with ExitStack() as st:
        wr = sb("wr", [P, 8, 2 * P])
        wT = sb("wT", [P, 2, 8, P])
        cell = sb("cell", [P, 2, C])
        cell0 = sb("cell0", [P, 2, C])
        xq = sb("xq", [P, 2, 8, C])
        H = halves[0][1]
        gate = [sb(f"gate{x}", [P, 8, H]) for x in range(2)]
        tig = [sb(f"tig{x}", [P, 2, H]) for x in range(2)]
        tfc = [sb(f"tfc{x}", [P, 2, H]) for x in range(2)]
        tc = [sb(f"tc{x}", [P, 2, H]) for x in range(2)]
        moved = sb("moved", [P, 2, 2, C - 1])
        oks = sb("oks", [P, 2])
        okf = sb("okf", [1, 1])
        flag = sb("flag", [1, 1], I32)
        psw = ps_("psw", [P, 2, 512])
        psg = [ps_(f"psg{x}", [P, 8, 64]) for x in range(2)]
        psk = ps_("psk", [P, 512])
        with nc.Block() as block:
            @block.sync
            def _(sp):
                sp.dma_start(wr[:], W_hh.rearrange("(g p) d -> p g d", p=P)).then_inc(S["w"], 16)

            @block.tensor
            def _(pe):
                pe.wait_ge(S["w"], 16)
                for n in range(8):
                    if n >= 2:
                        pe.wait_ge(S["wc"], n - 1)
                    for kk in range(2):
                        mm = pe.transpose(psw[:, n % 2, kk * P:(kk + 1) * P], wr[:, GATES[n], kk * P:(kk + 1) * P], k.ident[:])
                    mm.then_inc(S["wt"], 1)

            @block.vector
            def _(v):
                link = Chain(v, S["z"])
                for n in range(8):
                    v.wait_ge(S["wt"], n + 1)
                    v.tensor_copy(wT[:, :, n], psw[:, n % 2, 0:2 * P].rearrange("p (k t) -> p k t", k=2)).then_inc(S["wc"], 1)
                link(v.memset(k.hall[:, 0], 0.0))
                link(v.memset(cell[:], 0.0))
                link(v.memset(cell0[:], 0.0))

        sems = [S[n] for n in nm[3:] if n != "z"]

        def sweep():
            with nc.Block() as block:
                @block.sync
                def _(sp):
                    with sp.Fori(0, L // 2) as i:
                        for u in range(2):
                            s = 2 * i + u
                            rest(k, sp, S["ga0"], s + 1)
                            rest(k, sp, S["ga1"], s + 1)
                            sp.dma_start(xq[:, u], k.xp[bass.ds(s, 1)].rearrange("o p g c -> p (o g) c")
                                         ).then_inc(s_x[u], 16)

                @block.tensor
                def _(pe):
                    with pe.Fori(0, L) as s:
                        for x, (a, b) in enumerate(halves):
                            rest(k, pe, S[f"h{x}"], s + 1)
                            rest(k, pe, S[f"ga{x}"], s + 2)
                            for n in range(8):
                                for kk in range(2):
                                    mm = pe.matmul(psg[x][:, n, 0:b - a], wT[:, kk, n],
                                                   k.hall[:, bass.ds(s, 1), kk, a:b].rearrange("p o c -> p (o c)"),
                                                   start=(kk == 0), stop=(kk == 1))
                            mm.then_inc(S[f"mm{x}"], 1)

                @block.vector
                def _(v):
                    v.sem_inc(S["ga0"], 2)
                    v.sem_inc(S["ga1"], 2)
                    v.sem_inc(S["h0"], 1)
                    v.sem_inc(S["h1"], 1)

                    def add(i, u, x):
                        s, (a, b) = 2 * i + u, halves[x]
                        rest(k, v, s_x[u], 16 * (i + 1))
                        rest(k, v, S[f"h{x}"], s + 1)
                        rest(k, v, S[f"mm{x}"], s + 1)
                        v.tensor_tensor(gate[x][:, :, 0:b - a], psg[x][:, :, 0:b - a], xq[:, u, :, a:b], ALU.add
                                        ).then_inc(S[f"ga{x}"], 1)

                    def cells(i, u, x):
                        s, (a, b) = 2 * i + u, halves[x]
                        n = b - a
                        rest(k, v, S[f"sg{x}"], 2 * s + 2)
                        v.tensor_tensor(tfc[x][:, :, 0:n], gate[x][:, 2:4, 0:n], cell[:, :, a:b], ALU.mult)
                        v.tensor_tensor(tig[x][:, :, 0:n], gate[x][:, 0:2, 0:n], gate[x][:, 6:8, 0:n], ALU.mult
                                        ).then_inc(S[f"d{x}"], 1)
                        rest(k, v, S[f"d{x}"], s + 1)
                        v.tensor_tensor(cell[:, :, a:b], tfc[x][:, :, 0:n], tig[x][:, :, 0:n], ALU.add
                                        ).then_inc(S[f"cc{x}"], 1)

                    def state(i, u, x):
                        s, (a, b) = 2 * i + u, halves[x]
                        rest(k, v, S[f"tc{x}"], s + 1)
                        v.tensor_tensor(k.hall[:, bass.ds(s + 1, 1), :, a:b].rearrange("p o k c -> p (o k) c"),
                                        gate[x][:, 4:6, 0:b - a], tc[x][:, :, 0:b - a], ALU.mult
                                        ).then_inc(S[f"h{x}"], 1)

                    with v.Fori(0, L // 2) as i:
                        for u in range(2):
                            add(i, u, 0)
                            cells(i, u, 0)
                            add(i, u, 1)
                            state(i, u, 0)
                            cells(i, u, 1)
                            state(i, u, 1)

                @block.scalar
                def _(act):
                    act.activation(tc[0][:, 0, 0:1], k.zero[:, 0:1], ACT.Sigmoid)
                    act.activation(tc[0][:, 0, 1:2], k.zero[:, 0:1], ACT.Tanh).then_inc(S["e"], 1)
                    act.wait_ge(S["e"], 1)

                    def gates(s, x):
                        n = halves[x][1] - halves[x][0]
                        rest(k, act, S[f"ga{x}"], s + 3)
                        act.activation(gate[x][:, 0:6, 0:n], gate[x][:, 0:6, 0:n], ACT.Sigmoid).then_inc(S[f"sg{x}"], 1)
                        act.activation(gate[x][:, 6:8, 0:n], gate[x][:, 6:8, 0:n], ACT.Tanh).then_inc(S[f"sg{x}"], 1)

                    def cells(s, x):
                        a, b = halves[x]
                        rest(k, act, S[f"cc{x}"], s + 1)
                        act.activation(tc[x][:, :, 0:b - a], cell[:, :, a:b], ACT.Tanh).then_inc(S[f"tc{x}"], 1)

                    with act.Fori(0, L) as s:
                        gates(s, 0)
                        cells(s, 0)
                        gates(s, 1)
                        cells(s, 1)

            TOTAL = float(2 * 2 * (C - 1) * P)
            with nc.Block() as block:
                @block.vector
                def _(v):
                    link = Chain(v, S["q"])
                    link(v.tensor_tensor(moved[:, 0], k.hall[:, L, :, 0:C - 1], k.hall[:, 0, :, 1:C], ALU.subtract))
                    link(v.tensor_tensor(moved[:, 1], cell[:, :, 0:C - 1], cell0[:, :, 1:C], ALU.subtract))
                    link(v.tensor_tensor(moved[:], moved[:], moved[:], ALU.mult))
                    link(v.tensor_scalar(moved[:], moved[:], TOL * TOL, None, ALU.is_le))
                    link(v.tensor_reduce(oks[:, 0:1], moved[:].rearrange("p a k c -> p (a k c)"), AX, ALU.add))
                    v.wait_ge(S["pe"], 1)
                    link(v.tensor_scalar(okf[:], psk[0:1, 0:1], TOTAL - 0.5, None, ALU.is_lt))
                    link(v.tensor_copy(flag[:], okf[:]))
                    link(v.tensor_copy(cell0[:, :, 1:C], cell[:, :, 0:C - 1]))
                    link(v.tensor_copy(k.hnext[:], k.hall[:, L, :, 0:C - 1]))

                @block.tensor
                def _(pe):
                    pe.wait_ge(S["q"], 5)
                    pe.matmul(psk[0:1, 0:1], oks[:, 0:1], k.ones[:, 0:1], start=True, stop=True).then_inc(S["pe"], 1)
            clear(k, sems)

        def next_pass():
            with nc.Block() as block:
                @block.vector
                def _(v):
                    link = Chain(v, S["q"])
                    link(v.tensor_copy(k.hall[:, 0, :, 1:C], k.hnext[:]))
                    link(v.tensor_copy(cell[:], cell0[:]))
            clear(k, (S["q"],))
            sweep()

        sweep()
        with nc.Fori(0, FAST_PASSES - 1):
            next_pass()
        moving = lambda: nc.values_load(flag[0:1, 0:1], min_val=0, max_val=1) > 0
        with nc.If(moving()):
            with nc.Fori(0, C - FAST_PASSES):
                with nc.If(moving()):
                    next_pass()
                nc.all_engine_barrier()
        nc.all_engine_barrier()


def stage_output(k, W_lin, b_lin, fw, bw, out):
    nc, D, C, L = k.nc, k.D, k.C, k.L
    T = 2 * L
    NO = (C + 1) // 2
    nm = ("ha", "hb", "ld", "wt", "wc", "tp", "lg", "a", "s", "tot", "totc", "x0", "x1", "t2", "w", "pf", "q", "o0", "o1", "sm")
    S = {n: (k.pool_dma_sem if n in ("o0", "o1") else k.sem)("o_" + n) for n in nm}
    s_x, s_o = (S["x0"], S["x1"]), (S["o0"], S["o1"])
    with ExitStack() as st:
        sb = lambda n, s, d=F32: st.enter_context(nc.sbuf_tensor("o_" + n, s, d))
        ps_ = lambda n, s: st.enter_context(nc.psum_tensor("o_" + n, s, F32))
        wl, wlT = sb("wl", [2, D]), sb("wlT", [P, 2, 2])
        bl, fwb, bwb = sb("bl", [P, 2]), sb("fwb", [P, D]), sb("bwb", [P, D])
        lt = sb("lt", [P, 2])
        pickg = sb("pickg", [P, NO])
        run = sb("run", [P, D])
        totb = sb("totb", [P, D])
        w = sb("w_", [P, 2, D])
        xb, ob = sb("xb", [P, 2, D]), sb("ob", [P, 2, D])
        t1, t2 = sb("t1", [P, D]), sb("t2_", [P, D])
        hs = sb("hs", [P, 2, 2, T])
        psh, psl, psp, pss = ps_("psh", [P, 2, 512]), ps_("psl", [P, 2, 512]), ps_("psp", [P, 2, 512]), ps_("pss", [P, 512])
        A, B = 4, 8

        def copies(act, sem, used, per):
            def tile(m, n, u):
                hold(k, act, used, per * (m + 1))
                for kk in range(2):
                    ins = act.copy(hs[:, u, kk, 0:n * L].rearrange("p (c s) -> p c s", s=L),
                                   k.hall[:, 1:L + 1, kk, :].rearrange("p s c -> p c s")[:, bass.ds(2 * m, n), :])
                ins.then_inc(sem, 1)

            act.sem_inc(used, 2 * per)
            with act.Fori(0, NO // 2) as i:
                for u in range(2):
                    tile(2 * i + u, 2, u)
            tile(NO - 1, 1, 0)

        with nc.Block() as block:
            @block.sync
            def _(sp):
                sp.dma_start(wl[:], W_lin).then_inc(S["ld"], 16)
                sp.dma_start(bl[:], b_lin.partition_broadcast(P)).then_inc(S["ld"], 16)
                sp.dma_start(fwb[:], fw.rearrange("a d -> (a d)").partition_broadcast(P)).then_inc(S["ld"], 16)
                sp.dma_start(bwb[:], bw.rearrange("a d -> (a d)").partition_broadcast(P)).then_inc(S["ld"], 16)

            @block.tensor
            def _(pe):
                pe.wait_ge(S["ld"], 64)
                for kk in range(2):
                    mm = pe.transpose(psl[:, 0, kk * 2:kk * 2 + 2], wl[:, kk * P:(kk + 1) * P], k.ident[0:2, 0:2])
                mm.then_inc(S["wt"], 1)
                pe.wait_ge(S["wc"], 1)

                def tile(m, n, u):
                    rest(k, pe, S["ha"], m + 1)
                    rest(k, pe, S["s"], m + 1)
                    for kk in range(2):
                        mm = pe.transpose(psh[0:n * L, u, kk * P:(kk + 1) * P], hs[:, u, kk, 0:n * L], k.ident[:])
                    for kk in range(2):
                        mm = pe.matmul(psl[0:n * L, u, 0:2], hs[:, u, kk, 0:n * L], wlT[:, kk], start=(kk == 0), stop=(kk == 1))
                    mm.then_inc(S["lg"], 1)

                with pe.Fori(0, NO // 2) as i:
                    for u in range(2):
                        tile(2 * i + u, 2, u)
                tile(NO - 1, 1, 0)
                pe.wait_ge(S["s"], NO + 2)
                pe.matmul(pss[:, 0:D], k.ones[:], run[:], start=True, stop=True).then_inc(S["tot"], 1)

            @block.scalar
            def _(act):
                copies(act, S["ha"], S["lg"], 1)

            @block.vector
            def _(v):
                v.wait_ge(S["wt"], 1)
                v.tensor_copy(wlT[:].rearrange("p k l -> p (k l)"), psl[:, 0, 0:4]).then_inc(S["wc"], 1)
                link = Chain(v, S["sm"])
                link(v.memset(run[:], 0.0))
                v.sem_inc(S["s"], 2)

                def tile(m, n, u):
                    r = n * L
                    rest(k, v, S["lg"], m + 3)
                    link = Chain(v, S["a"], k, m * A)
                    link(v.tensor_tensor(lt[0:r], psl[0:r, u, 0:2], bl[0:r], ALU.add))
                    g = pickg[0:r, bass.ds(m, 1)]
                    link(v.tensor_tensor(g, lt[0:r, 1:2], lt[0:r, 0:1], ALU.is_gt))
                    link(v.tensor_scalar(t1[0:r], psh[0:r, u, 0:D], g, None, ALU.mult))
                    link(v.tensor_tensor(run[0:r], run[0:r], t1[0:r], ALU.add))
                    v.sem_inc(S["s"], 1)

                with v.Fori(0, NO // 2) as i:
                    for u in range(2):
                        tile(2 * i + u, 2, u)
                tile(NO - 1, 1, 0)
                v.wait_ge(S["tot"], 1)
                v.tensor_tensor(totb[:], pss[:, 0:D], bwb[:], ALU.mult).then_inc(S["totc"], 1)
                v.tensor_tensor(fwb[:], fwb[:], bwb[:], ALU.subtract).then_inc(S["totc"], 1)
                v.memset(run[:], 0.0).then_inc(S["totc"], 1)
                v.wait_ge(S["totc"], 3)

        with nc.Block() as block:
            @block.sync
            def _(sp):
                def tile(m, n, u, j):
                    rest(k, sp, S["q"], B * m + 1)
                    sp.dma_start(xb[0:n * L, u], k.x3[bass.ds(m * T, n * L)]).then_inc(s_x[u], 16)
                with sp.Fori(0, NO // 2) as i:
                    for u in range(2):
                        tile(2 * i + u, 2, u, i)
                tile(NO - 1, 1, 0, NO // 2)

            @block.gpsimd
            def _(pool):
                prime(k, pool, s_o)

                def tile(m, n, u):
                    hold(k, pool, S["q"], B * (m + 1) + 1)
                    pool.dma_start(out[bass.ds(m * T, n * L)], ob[0:n * L, u]).then_inc(s_o[u], 16)
                with pool.Fori(0, NO // 2) as i:
                    for u in range(2):
                        tile(2 * i + u, 2, u)
                tile(NO - 1, 1, 0)
                pool.wait_ge(s_o[0], 16 * (NO // 2 + 2))
                pool.wait_ge(s_o[1], 16 * (NO // 2 + 1))

            @block.tensor
            def _(pe):
                def tile(m, n, u):
                    r = n * L
                    rest(k, pe, S["hb"], m + 1)
                    rest(k, pe, S["q"], B * m + 1)
                    for kk in range(2):
                        mm = pe.transpose(psh[0:r, u, kk * P:(kk + 1) * P], hs[:, u, kk, 0:r], k.ident[:])
                    mm.then_inc(S["t2"], 1)
                    rest(k, pe, S["w"], m + 1)
                    pe.matmul(psp[0:r, u, 0:D], k.ones[:, 0:r], run[:], start=True, stop=False)
                    pe.matmul(psp[0:r, u, 0:D], k.strict[0:r, 0:r], w[0:r, u], start=False, stop=True).then_inc(S["pf"], 1)
                with pe.Fori(0, NO // 2) as i:
                    for u in range(2):
                        tile(2 * i + u, 2, u)
                tile(NO - 1, 1, 0)

            @block.scalar
            def _(act):
                copies(act, S["hb"], S["t2"], 1)

            @block.vector
            def _(v):
                v.sem_inc(S["q"], 1)

                def tile(m, n, u, i):
                    r = n * L
                    link = Chain(v, S["q"], k, m * B + 1)
                    rest(k, v, S["t2"], m + 3)
                    link(v.tensor_scalar(w[0:r, u], psh[0:r, u, 0:D], pickg[0:r, bass.ds(m, 1)], None, ALU.mult))
                    v.sem_inc(S["w"], 1)
                    rest(k, v, s_x[u], 16 * (i + 1))
                    rest(k, v, s_o[u], 16 * (i + 1))
                    link(v.scalar_tensor_tensor(out=t1[0:r], in0=psh[0:r, u, 0:D], scalar=2.0, in1=xb[0:r, u],
                                                op0=ALU.mult, op1=ALU.add))
                    link(v.tensor_tensor(t2[0:r], w[0:r, u], bwb[0:r], ALU.mult))
                    link(v.tensor_tensor(t1[0:r], t1[0:r], t2[0:r], ALU.subtract))
                    link(v.tensor_tensor(t1[0:r], t1[0:r], totb[0:r], ALU.add))
                    rest(k, v, S["pf"], m + 1)
                    link(v.tensor_tensor(t2[0:r], psp[0:r, u, 0:D], fwb[0:r], ALU.mult))
                    link(v.tensor_tensor(run[0:r], run[0:r], w[0:r, u], ALU.add))
                    link(v.tensor_tensor(ob[0:r, u], t1[0:r], t2[0:r], ALU.add))
                with v.Fori(0, NO // 2) as i:
                    for u in range(2):
                        tile(2 * i + u, 2, u, i)
                tile(NO - 1, 1, 0, NO // 2)


def gnn_moe_gcn_lstm(nc, x, src, dst, edge_type_16, L0_gnn_W_r, L0_gnn_W0_w, L0_gnn_W0_b, L0_ffn_gate_w,
                     L0_ffn_gate_b, L0_ffn_w1, L0_ffn_b1, L0_ffn_w2, L0_ffn_b2, L1_gnn_W, L1_gnn_b, L1_ffn_W_ih,
                     L1_ffn_W_hh, L1_ffn_b_ih, L1_ffn_b_hh, L1_ffn_W_lin, L1_ffn_b_lin, L1_ffn_fw_att,
                     L1_ffn_bw_att, out):
    k = K()
    k.nc = nc
    k.N, k.D = x.shape
    k.E = src.shape[0]
    k.R = L0_gnn_W_r.shape[0]
    k.EX = L0_ffn_gate_w.shape[1]
    k.NT = -(-k.N // P)
    k.NT += k.NT % 2
    k.NP = k.NT * P
    k.NG = -(-k.E // EG)
    assert k.NG % 2 == 0 and k.D == 2 * P
    k.CAP = -(-5 * k.N // (4 * k.EX))
    k.CS = -(-k.CAP // 512) * 512
    k.C, k.L = 125, k.N // 125
    assert k.C * k.L == k.N and k.L % 2 == 0
    with ExitStack() as ctx:
        k.stage_sems, k.pool_dma_sems, k.pool_dma_used = [], [], 0
        sb = lambda n, s, d=F32: ctx.enter_context(nc.sbuf_tensor("k_" + n, s, d))
        dram = lambda n, s, d=F32: nc.dram_tensor("scratch_" + n, s, d, **k_kinds.get(n, {})).ap()
        k.s_seen, k.s_win = (ctx.enter_context(nc.semaphore(n)) for n in ("seen", "win"))
        k.xpad, k.x1, k.x2, k.x3, k.gtab = (dram(n, (k.NP, k.D)) for n in ("xpad", "x1", "x2", "x3", "gtab"))
        k.primed, k.n_primed = dram("primed", (64, 16)), 0
        k.typ = dram("typ", (k.NG * EG,), I32)
        k.hrel = dram("hrel", (k.NP, k.R * k.D))
        k.buf = dram("buf", (k.EX * k.CS + k.NP, k.D))
        k.ybuf = dram("ybuf", (k.EX * k.CS, k.D))
        k.xp = dram("xp", (k.L, P, 8, k.C))
        k.iota_i, k.part_i = sb("iota_i", [P, P], I32), sb("part_i", [P, 1], I32)
        k.iota, k.part = sb("iota", [P, P]), sb("part", [P, 1])
        k.ones, k.zero, k.ident, k.upper, k.strict = (sb(n, [P, P]) for n in ("ones", "zero", "ident", "upper", "strict"))
        k.dinv, k.gate = sb("dinv", [P, k.NT]), sb("gate", [P, k.NT])
        k.slot_read, k.slot_write = sb("slot_read", [P, k.NT], I32), sb("slot_write", [P, k.NT], I32)
        k.islot = sb("islot", [P, 2], I32)
        k.eps = sb("eps", [P, 1])
        k.scattered = sb("scattered", [1, 1], I32)
        stage_constants(k)
        k.end_stage()
        with ExitStack() as graph:
            gs = lambda n, s, d=F32: graph.enter_context(nc.sbuf_tensor("k_" + n, s, d))
            k.accT = gs("accT", [P, 2, k.NP])
            with ExitStack() as edges:
                es = lambda n, s, d=F32: edges.enter_context(nc.sbuf_tensor("k_" + n, s, d))
                k.dstf, k.rel, k.typf = (es(n, [P, k.NG, PER]) for n in ("dstf", "rel", "typf"))
                k.src_row, k.rel_row = (es(n, [P, k.NG, PER], I32) for n in ("src_row", "rel_row"))
                k.base = es("base", [1, k.NG], I32)
                k.win_i, k.win_f = es("win_i", [P, 1], I32), es("win_f", [P, 1])
                stage_edges(k, x, src, dst, edge_type_16)
                k.end_stage()
                with ExitStack() as first:
                    k.degT = first.enter_context(nc.sbuf_tensor("k_degT", [k.R, k.NP], F32))
                    stage_degrees(k)
                    k.end_stage()
                    stage_relations(k, L0_gnn_W_r, L0_gnn_W0_w, L0_gnn_W0_b)
                    k.end_stage()
                    table = k.hrel.rearrange("n (r d) -> (n r) d", r=k.R)
                    stage_gather(k, "a_", table, k.rel_row, True)
                    k.end_stage()
                stage_route(k, L0_ffn_gate_w, L0_ffn_gate_b)
                k.end_stage()
                stage_experts(k, L0_ffn_w1, L0_ffn_b1, L0_ffn_w2, L0_ffn_b2)
                k.end_stage()
                stage_combine(k, L1_gnn_W)
                k.end_stage()
                stage_gather(k, "b_", k.gtab, k.src_row, False)
                k.end_stage()
            stage_x3(k, L1_gnn_b)
            k.end_stage()
            stage_inputs(k, L1_ffn_W_ih, L1_ffn_b_ih, L1_ffn_b_hh)
            k.end_stage()
        k.hnext = sb("hnext", [P, 2, k.C - 1])
        stage_lstm(k, ctx, L1_ffn_W_hh)
        k.end_stage()
        stage_output(k, L1_ffn_W_lin, L1_ffn_b_lin, L1_ffn_fw_att, L1_ffn_bw_att, out)
        k.end_stage()


k_kinds = {}

_INS = ['x', 'src', 'dst', 'edge_type_16', 'L0_gnn_W_r', 'L0_gnn_W0_w', 'L0_gnn_W0_b', 'L0_ffn_gate_w',
        'L0_ffn_gate_b', 'L0_ffn_w1', 'L0_ffn_b1', 'L0_ffn_w2', 'L0_ffn_b2', 'L1_gnn_W', 'L1_gnn_b', 'L1_ffn_W_ih',
        'L1_ffn_W_hh', 'L1_ffn_b_ih', 'L1_ffn_b_hh', 'L1_ffn_W_lin', 'L1_ffn_b_lin', 'L1_ffn_fw_att',
        'L1_ffn_bw_att']
_OUTS = [((6250, 256), 'float32')]


def kernel(**inputs):
    import numpy as _np
    import concourse.bacc as _bacc
    from concourse import mybir as _mybir
    from concourse.bass_utils import run_bass_kernel_spmd as _run

    nc = _bacc.Bacc("TRN2", target_bir_lowering=False, num_devices=1)
    arrays, args = {}, []
    for name in _INS:
        a = _np.ascontiguousarray(inputs[name])
        arrays[f"in_{name}_dram"] = a
        args.append(nc.dram_tensor(f"in_{name}_dram", a.shape, _mybir.dt.from_np(a.dtype), kind="ExternalInput").ap())
    for i, (shape, dtype) in enumerate(_OUTS):
        dt = _mybir.dt.from_np(_np.dtype(dtype))
        args.append(nc.dram_tensor(f"out_{i}_dram", shape, dt, kind="ExternalOutput").ap())
    gnn_moe_gcn_lstm(nc, *args)
    r = _run(nc, [arrays], core_ids=[0])
    got = tuple(r.results[0][f"out_{i}_dram"] for i in range(len(_OUTS)))
    return got[0]
```
